# Optimizing a Trainium2 kernel written in Bass

```python
import numpy as np
import jax
import jax.numpy as jnp

def _softmax(x, axis=-1):
    return jax.nn.softmax(x, axis=axis)

def _gelu(x):
    return jax.nn.gelu(x, approximate=True)

def _silu(x):
    return jax.nn.silu(x)

def _sigmoid(x):
    return jax.nn.sigmoid(x)

def _layernorm(x, axis=-1, eps=1e-05):
    m = jnp.mean(x, axis=axis, keepdims=True)
    v = jnp.var(x, axis=axis, keepdims=True)
    return (x - m) / jnp.sqrt(v + eps)

def _scatter_add(tgt, idx, src, axis=0):
    return tgt.at[idx].add(src)

def _segment_sum(src, seg, n):
    return jax.ops.segment_sum(src, seg, n)
kernel_name = 'mk_decoder_preln_d4_seqx_r8_e6031a'

def setup_inputs(seed: int=0):
    np.random.seed(seed)
    _w = jnp.asarray

    def _rec_inputs():
        import jax
        import jax.numpy as jnp
        _rk = jax.random.key(seed)
        x = -0.000125 + 0.9999 * jax.random.normal(jax.random.fold_in(_rk, 1), (32, 128, 128), jnp.float32)
        _lenS = 128 - jax.random.randint(jax.random.fold_in(_rk, 7), (32,), 0, max(1, 128 // 4) + 1, jnp.int32)
        _lenS2 = 128 - jax.random.randint(jax.random.fold_in(_rk, 8), (32,), 0, max(1, 128 // 4) + 1, jnp.int32)
        _ctx_1024P = jax.random.normal(jax.random.fold_in(_rk, 11), (32, 16, 128), jnp.float32)
        _ctx_1024c = jax.random.dirichlet(jax.random.fold_in(_rk, 511), 0.3 * jnp.ones((16,), jnp.float32), (32, 128))
        _ctx_1024t = jnp.einsum('bsk,bkd->bsd', _ctx_1024c, _ctx_1024P)
        _ctx_1024t = _ctx_1024t * jax.lax.rsqrt(jnp.mean(jnp.square(_ctx_1024t)) + 1e-12) * 0.953939
        ctx_1024 = -1.52775e-05 + 0.999936 * (_ctx_1024t + 0.3 * jax.random.normal(jax.random.fold_in(_rk, 611), (32, 128, 128), jnp.float32))
        _validS = jnp.arange(128)[None, :] < _lenS[:, None]
        _validS2 = jnp.arange(128)[None, :] < _lenS2[:, None]
        _causal = jnp.tril(jnp.ones((128, 128), dtype=bool))
        mask_Bx1xSxS2_ik1 = jnp.where(jnp.broadcast_to(_validS2[:, None, None, :], (32, 1, 128, 128)), 1, 0).astype(jnp.int32)
        return (x, ctx_1024, mask_Bx1xSxS2_ik1)
    x, ctx_1024, mask_Bx1xSxS2_ik1 = _rec_inputs()

    def _L0_attn_setup():
        import jax, jax.numpy as jnp
        import numpy as np
        B, T, C = (4, 512, 128)
        H = 16
        D = C // H
        W_SCALE = 0.02
        key = jax.random.key(seed)
        ks = jax.random.split(key, 9)
        inp = {'x': jax.random.normal(ks[0], (B, T, C), dtype=jnp.float32)}
        for i, nm in enumerate(['q', 'k', 'v', 'o']):
            inp[f'W{nm}'] = jax.random.normal(ks[1 + i], (C, C), dtype=jnp.float32) * W_SCALE
            inp[f'b{nm}'] = jnp.zeros((C,), dtype=jnp.float32)
        return inp
    _L0_attn_all = _L0_attn_setup()
    _L0_attn_in = {k: v for k, v in _L0_attn_all.items() if k in ('Wq', 'bq', 'Wk', 'bk', 'Wv', 'bv', 'Wo', 'bo')}
    del _L0_attn_all

    def _L0_xattn_setup():
        import jax, jax.numpy as jnp
        import numpy as np
        DECAY = 0.9
        key = jax.random.key(seed)
        k1, k2, k3 = jax.random.split(key, 3)
        B, S, D = (8, 512, 128)
        q = jax.random.normal(k1, (B, S, D), dtype=jnp.float32)
        k = jax.random.normal(k2, (B, S, D), dtype=jnp.float32)
        v = jax.random.normal(k3, (B, S, D), dtype=jnp.float32)
        return {'q': q, 'k': k, 'v': v}
    _L0_xattn_all = _L0_xattn_setup()
    _L0_xattn_in = {k: v for k, v in _L0_xattn_all.items() if k in ()}
    del _L0_xattn_all

    def _L0_ffn_setup():
        import jax, jax.numpy as jnp
        import numpy as np
        BLOCK = 16
        _GRID = jnp.array([0.0, 0.5, 1.0, 1.5, 2.0, 3.0, 4.0, 6.0], dtype=jnp.float32)
        _MID = jnp.array([0.25, 0.75, 1.25, 1.75, 2.5, 3.5, 5.0], dtype=jnp.float32)

        def fp4_quant_dequant(x):
            shape = x.shape
            xb = x.reshape(shape[:-1] + (shape[-1] // BLOCK, BLOCK))
            scale = jnp.max(jnp.abs(xb), axis=-1, keepdims=True) / 6.0
            scale = jnp.maximum(scale, jnp.float32(1e-12))
            xn = xb / scale
            idx = jnp.searchsorted(_MID, jnp.abs(xn))
            q = _GRID[idx] * jnp.sign(xn) * scale
            return q.reshape(shape)

        def fp4_linear(x, w):
            xq = fp4_quant_dequant(x)
            wq = fp4_quant_dequant(w)
            return jnp.einsum('bsk,nk->bsn', xq, wq)
        key = jax.random.key(seed)
        k1, k2, k3, k4 = jax.random.split(key, 4)
        H, I = (128, 352)
        x = jax.random.normal(k1, (4, 512, H), dtype=jnp.float32)
        w_gate = jax.random.normal(k2, (I, H), dtype=jnp.float32) * 0.02
        w_up = jax.random.normal(k3, (I, H), dtype=jnp.float32) * 0.02
        w_down = jax.random.normal(k4, (H, I), dtype=jnp.float32) * 0.02
        return {'x': x, 'w_gate': w_gate, 'w_up': w_up, 'w_down': w_down}
    _L0_ffn_all = _L0_ffn_setup()
    _L0_ffn_in = {k: v for k, v in _L0_ffn_all.items() if k in ('w_gate', 'w_up', 'w_down')}
    del _L0_ffn_all

    def _L1_attn_setup():
        import jax, jax.numpy as jnp
        import numpy as np
        B, T, D = (2, 512, 128)
        H, HD = (16, 64)
        KV = H * HD

        def _l2norm(t, eps=1e-06):
            return t * jax.lax.rsqrt(jnp.sum(t * t, axis=-1, keepdims=True) + eps)
        key = jax.random.key(seed)
        ks = jax.random.split(key, 6)
        sc = lambda k, shape, s: jax.random.normal(k, shape, jnp.float32) * s
        return {'x': sc(ks[0], (B, T, D), 1.0), 'W_in': sc(ks[1], (D, 4 * KV), D ** (-0.5)), 'W_ba': sc(ks[2], (D, 2 * H), D ** (-0.5)), 'conv_w': sc(ks[3], (3 * KV, 1, 4), 0.5), 'dt_bias': jnp.ones((H,), jnp.float32), 'A_log': jnp.log(jax.random.uniform(ks[4], (H,), jnp.float32, 0.001, 16.0)), 'norm_w': jnp.ones((HD,), jnp.float32), 'W_o': sc(ks[5], (KV, D), KV ** (-0.5))}
    _L1_attn_all = _L1_attn_setup()
    _L1_attn_in = {k: v for k, v in _L1_attn_all.items() if k in ('W_in', 'W_ba', 'conv_w', 'dt_bias', 'A_log', 'norm_w', 'W_o')}
    del _L1_attn_all

    def _L1_xattn_setup():
        import jax, jax.numpy as jnp
        import numpy as np
        EMBED_DIM = 128
        NUM_HEADS = 16
        HEAD_DIM = EMBED_DIM // NUM_HEADS
        SCALE = HEAD_DIM ** (-0.5)
        B, NQ, NK = (2, 256, 256)
        key = jax.random.key(seed)
        ks = jax.random.split(key, 12)
        s = 1.0 / np.sqrt(EMBED_DIM)
        inp = {'query': jax.random.normal(ks[0], (B, NQ, EMBED_DIM), jnp.float32), 'key': jax.random.normal(ks[1], (B, NK, EMBED_DIM), jnp.float32), 'value': jax.random.normal(ks[2], (B, NK, EMBED_DIM), jnp.float32), 'mask': jax.random.randint(ks[3], (B, 1, NQ, NK), 0, 2, jnp.int32), 'Wq': jax.random.normal(ks[4], (EMBED_DIM, EMBED_DIM), jnp.float32) * s, 'bq': jnp.zeros((EMBED_DIM,), jnp.float32), 'Wk': jax.random.normal(ks[5], (EMBED_DIM, EMBED_DIM), jnp.float32) * s, 'bk': jnp.zeros((EMBED_DIM,), jnp.float32), 'Wv': jax.random.normal(ks[6], (EMBED_DIM, EMBED_DIM), jnp.float32) * s, 'bv': jnp.zeros((EMBED_DIM,), jnp.float32), 'Wo': jax.random.normal(ks[7], (EMBED_DIM, EMBED_DIM), jnp.float32) * s, 'bo': jnp.zeros((EMBED_DIM,), jnp.float32)}
        return inp
    _L1_xattn_all = _L1_xattn_setup()
    _L1_xattn_in = {k: v for k, v in _L1_xattn_all.items() if k in ('Wq', 'bq', 'Wk', 'bk', 'Wv', 'bv', 'Wo', 'bo')}
    del _L1_xattn_all

    def _L1_ffn_setup():
        import jax, jax.numpy as jnp
        import numpy as np
        B, T, D, DFF, E = (4, 256, 128, 512, 8)
        key = jax.random.key(seed)
        ks = jax.random.split(key, 4)
        s_in = 1.0 / np.sqrt(D)
        s_ff = 1.0 / np.sqrt(DFF)
        return {'x': jax.random.normal(ks[0], (B, T, D), dtype=jnp.float32), 'gate_W': jax.random.normal(ks[1], (D, E), dtype=jnp.float32) * s_in, 'gate_b': jnp.zeros((E,), dtype=jnp.float32), 'W1': jax.random.normal(ks[2], (E, D, DFF), dtype=jnp.float32) * s_in, 'b1': jnp.zeros((E, DFF), dtype=jnp.float32), 'W2': jax.random.normal(ks[3], (E, DFF, D), dtype=jnp.float32) * s_ff, 'b2': jnp.zeros((E, D), dtype=jnp.float32)}
    _L1_ffn_all = _L1_ffn_setup()
    _L1_ffn_in = {k: v for k, v in _L1_ffn_all.items() if k in ('gate_W', 'gate_b', 'W1', 'b1', 'W2', 'b2')}
    del _L1_ffn_all

    def _L2_attn_setup():
        import jax, jax.numpy as jnp
        import numpy as np
        from jax import lax
        H = 128
        EXPAND = 2
        I = EXPAND * H
        N = 16
        K = 4
        R = 64
        EPS = 1e-06
        B_SZ, L = (2, 128)

        def rmsnorm(x, w):
            v = jnp.mean(x.astype(jnp.float32) ** 2, axis=-1, keepdims=True)
            return w * (x * jax.lax.rsqrt(v + EPS)).astype(x.dtype)
        key = jax.random.key(seed)
        ks = jax.random.split(key, 10)
        s = 0.02
        inp = {'hidden_states': jax.random.normal(ks[0], (B_SZ, L, H), jnp.float32), 'in_proj_w': jax.random.normal(ks[1], (2 * I, H), jnp.float32) * s, 'conv_w': jax.random.normal(ks[2], (I, 1, K), jnp.float32) * s, 'conv_b': jnp.zeros((I,), jnp.float32), 'x_proj_w': jax.random.normal(ks[3], (R + 2 * N, I), jnp.float32) * s, 'dt_proj_w': jax.random.normal(ks[4], (I, R), jnp.float32) * s, 'dt_proj_b': jax.random.normal(ks[5], (I,), jnp.float32) * 0.1, 'dt_ln_w': jnp.ones((R,), jnp.float32), 'b_ln_w': jnp.ones((N,), jnp.float32), 'c_ln_w': jnp.ones((N,), jnp.float32), 'A_log': jnp.log(jnp.broadcast_to(jnp.arange(1, N + 1, dtype=jnp.float32)[None, :], (I, N))), 'D': jnp.ones((I,), jnp.float32), 'out_proj_w': jax.random.normal(ks[6], (H, I), jnp.float32) * s}
        return inp
    _L2_attn_all = _L2_attn_setup()
    _L2_attn_in = {k: v for k, v in _L2_attn_all.items() if k in ('in_proj_w', 'conv_w', 'conv_b', 'x_proj_w', 'dt_proj_w', 'dt_proj_b', 'dt_ln_w', 'b_ln_w', 'c_ln_w', 'A_log', 'D', 'out_proj_w')}
    del _L2_attn_all

    def _L2_xattn_setup():
        import jax, jax.numpy as jnp
        import numpy as np
        B, SQ, SV, D = (8, 256, 256, 128)
        key = jax.random.key(seed)
        kq, kv = jax.random.split(key)
        query = jax.random.normal(kq, (B, SQ, D), dtype=jnp.float32)
        value = jax.random.normal(kv, (B, SV, D), dtype=jnp.float32)
        return {'query': query, 'value': value}
    _L2_xattn_all = _L2_xattn_setup()
    _L2_xattn_in = {k: v for k, v in _L2_xattn_all.items() if k in ()}
    del _L2_xattn_all

    def _L2_ffn_setup():
        import jax, jax.numpy as jnp
        import numpy as np
        from math import ceil
        CAPACITY_FACTOR = 2.0
        MIN_CAPACITY = 4
        key = jax.random.key(seed)
        ks = jax.random.split(key, 4)
        B, S, D, Di, E = (4, 256, 128, 512, 8)
        x = jax.random.normal(ks[0], (B, S, D), dtype=jnp.float32)
        Wr = jax.random.normal(ks[1], (D, E), dtype=jnp.float32) * D ** (-0.5)
        W1 = jax.random.normal(ks[2], (E, D, Di), dtype=jnp.float32) * D ** (-0.5)
        b1 = jnp.zeros((E, Di), dtype=jnp.float32)
        W2 = jax.random.normal(ks[3], (E, Di, D), dtype=jnp.float32) * Di ** (-0.5)
        b2 = jnp.zeros((E, D), dtype=jnp.float32)
        return {'x': x, 'Wr': Wr, 'W1': W1, 'b1': b1, 'W2': W2, 'b2': b2}
    _L2_ffn_all = _L2_ffn_setup()
    _L2_ffn_in = {k: v for k, v in _L2_ffn_all.items() if k in ('Wr', 'W1', 'b1', 'W2', 'b2')}
    del _L2_ffn_all

    def _L3_attn_setup():
        import jax, jax.numpy as jnp
        import numpy as np
        N_HEAD = 16
        EPS = 1e-06

        def _linear_attention(q, k, v):
            B, H, D = (q.shape[1], q.shape[2], q.shape[3])

            def step(carry, qkv_t):
                S, z = carry
                qt, kt, vt = qkv_t
                S = S + kt[..., :, None] * vt[..., None, :]
                z = z + kt
                num = jnp.einsum('bhi,bhij->bhj', qt, S)
                den = jnp.sum(qt * z, axis=-1, keepdims=True)
                return ((S, z), num / (den + EPS))
            S0 = jnp.zeros((B, H, D, D), q.dtype)
            z0 = jnp.zeros((B, H, D), q.dtype)
            _, y = jax.lax.scan(step, (S0, z0), (q, k, v))
            return y
        key = jax.random.key(seed)
        k1, k2, k3 = jax.random.split(key, 3)
        B, T, C = (2, 256, 128)
        x = jax.random.normal(k1, (B, T, C), dtype=jnp.float32)
        w_attn = jax.random.normal(k2, (C, 3 * C), dtype=jnp.float32) * 0.02
        w_proj = jax.random.normal(k3, (C, C), dtype=jnp.float32) * 0.02
        return {'x': x, 'w_attn': w_attn, 'w_proj': w_proj}
    _L3_attn_all = _L3_attn_setup()
    _L3_attn_in = {k: v for k, v in _L3_attn_all.items() if k in ('w_attn', 'w_proj')}
    del _L3_attn_all

    def _L3_xattn_setup():
        import jax, jax.numpy as jnp
        import numpy as np
        EPS = 1e-08
        LN_EPS = 1e-05

        def _layernorm(x, g, b):
            mu = jnp.mean(x, axis=-1, keepdims=True)
            var = jnp.var(x, axis=-1, keepdims=True)
            return (x - mu) * jax.lax.rsqrt(var + LN_EPS) * g + b

        def _prob(x):
            x = jnp.tanh(x) * 0.499 + 0.5
            return jnp.clip(x / (jnp.sum(x, axis=-1, keepdims=True) + EPS), EPS)
        key = jax.random.key(seed)
        ks = jax.random.split(key, 8)
        B, N, D = (8, 256, 128)
        H = 4 * D
        s = 0.02
        return {'q': jax.random.normal(ks[0], (B, N, D), jnp.float32), 'k': jax.random.normal(ks[1], (B, N, D), jnp.float32), 'v': jax.random.normal(ks[2], (B, N, D), jnp.float32), 'W_diff': jax.random.normal(ks[3], (D, D), jnp.float32) * s, 'b_diff': jnp.zeros((D,), jnp.float32), 'ln_g': jnp.ones((D,), jnp.float32), 'ln_b': jnp.zeros((D,), jnp.float32), 'W1': jax.random.normal(ks[4], (H, D), jnp.float32) * s, 'b1': jnp.zeros((H,), jnp.float32), 'W2': jax.random.normal(ks[5], (D, H), jnp.float32) * s, 'b2': jnp.zeros((D,), jnp.float32)}
    _L3_xattn_all = _L3_xattn_setup()
    _L3_xattn_in = {k: v for k, v in _L3_xattn_all.items() if k in ('W_diff', 'b_diff', 'ln_g', 'ln_b', 'W1', 'b1', 'W2', 'b2')}
    del _L3_xattn_all

    def _L3_ffn_setup():
        import jax, jax.numpy as jnp
        import numpy as np
        B, T, N = (2, 256, 128)
        H = 16
        E = 8
        K = 2
        FF = 4 * N
        EPS = 1e-05
        SCALE = 1.0

        def _layernorm(x, scale, bias):
            mu = x.mean(-1, keepdims=True)
            var = ((x - mu) ** 2).mean(-1, keepdims=True)
            return (x - mu) * jax.lax.rsqrt(var + EPS) * scale + bias

        def _attention(x, w_qkv, b_qkv, w_proj, b_proj):
            b, t, n = x.shape
            qkv = x @ w_qkv + b_qkv
            q, k, v = jnp.split(qkv, 3, axis=2)
            hd = n // H
            q = q.reshape(b, t, H, hd).transpose(0, 2, 1, 3)
            k = k.reshape(b, t, H, hd).transpose(0, 2, 1, 3)
            v = v.reshape(b, t, H, hd).transpose(0, 2, 1, 3)
            att = jnp.einsum('bhqd,bhkd->bhqk', q, k) / hd ** 0.5
            mask = jnp.tril(jnp.ones((1, 1, t, t), bool))
            att = jnp.where(mask, att, jnp.finfo(jnp.float32).min)
            att = jax.nn.softmax(att, axis=-1)
            y = jnp.einsum('bhqk,bhkd->bhqd', att, v)
            y = y.transpose(0, 2, 1, 3).reshape(b, t, n)
            return y @ w_proj + b_proj

        def _moe(x, w_gate, b_gate, w_fc, b_fc, w_fcproj, b_fcproj):
            b, t, n = x.shape
            xf = x.reshape(-1, n)
            bt = xf.shape[0]
            logits = xf @ w_gate + b_gate
            probs = jax.nn.softmax(logits, axis=-1)
            top_p, top_i = jax.lax.top_k(probs, K)
            out = jnp.zeros((bt, n), xf.dtype)
            expert_mask = jnp.transpose(jax.nn.one_hot(top_i, E), (2, 1, 0))
            rows = jnp.arange(bt)
            for e in range(E):
                active = expert_mask[e]
                mask = active.any(axis=0)
                cumsum = jnp.cumsum(mask) - 1
                indices = jnp.where(mask, cumsum, -1)
                sel = jnp.where(mask[:, None], xf, 0.0)
                h = jax.nn.gelu(sel @ w_fc[e] + b_fc[e], approximate=True)
                eo = h @ w_fcproj[e] + b_fcproj[e]
                rp = jnp.where(mask[:, None], top_p[rows, jnp.argmax(active, axis=0)][:, None], 0.0)
                out = out.at[indices].add(eo * rp)
            return out.reshape(b, t, n)
        key = jax.random.key(seed)
        ks = jax.random.split(key, 12)
        s = lambda fan_in: 1.0 / np.sqrt(fan_in)
        return {'x': jax.random.normal(ks[0], (B, T, N), jnp.float32), 'ln1_scale': jnp.ones((N,), jnp.float32), 'ln1_bias': jnp.zeros((N,), jnp.float32), 'w_qkv': jax.random.normal(ks[1], (N, 3 * N), jnp.float32) * s(N), 'b_qkv': jnp.zeros((3 * N,), jnp.float32), 'w_attnproj': jax.random.normal(ks[2], (N, N), jnp.float32) * s(N), 'b_attnproj': jnp.zeros((N,), jnp.float32), 'ln2_scale': jnp.ones((N,), jnp.float32), 'ln2_bias': jnp.zeros((N,), jnp.float32), 'w_gate': jax.random.normal(ks[3], (N, E), jnp.float32) * s(N), 'b_gate': jnp.zeros((E,), jnp.float32), 'w_fc': jax.random.normal(ks[4], (E, N, FF), jnp.float32) * s(N), 'b_fc': jnp.zeros((E, FF), jnp.float32), 'w_fcproj': jax.random.normal(ks[5], (E, FF, N), jnp.float32) * s(FF), 'b_fcproj': jnp.zeros((E, N), jnp.float32)}
    _L3_ffn_all = _L3_ffn_setup()
    _L3_ffn_in = {k: v for k, v in _L3_ffn_all.items() if k in ('ln1_scale', 'ln1_bias', 'w_qkv', 'b_qkv', 'w_attnproj', 'b_attnproj', 'ln2_scale', 'ln2_bias', 'w_gate', 'b_gate', 'w_fc', 'b_fc', 'w_fcproj', 'b_fcproj')}
    del _L3_ffn_all
    return {'x': x, 'ctx_1024': ctx_1024, 'mask_Bx1xSxS2_ik1': mask_Bx1xSxS2_ik1, 'L0_attn_Wq': _L0_attn_in['Wq'], 'L0_attn_bq': _L0_attn_in['bq'], 'L0_attn_Wk': _L0_attn_in['Wk'], 'L0_attn_bk': _L0_attn_in['bk'], 'L0_attn_Wv': _L0_attn_in['Wv'], 'L0_attn_bv': _L0_attn_in['bv'], 'L0_attn_Wo': _L0_attn_in['Wo'], 'L0_attn_bo': _L0_attn_in['bo'], 'L0_ffn_w_gate': _L0_ffn_in['w_gate'], 'L0_ffn_w_up': _L0_ffn_in['w_up'], 'L0_ffn_w_down': _L0_ffn_in['w_down'], 'L1_attn_W_in': _L1_attn_in['W_in'], 'L1_attn_W_ba': _L1_attn_in['W_ba'], 'L1_attn_conv_w': _L1_attn_in['conv_w'], 'L1_attn_dt_bias': _L1_attn_in['dt_bias'], 'L1_attn_A_log': _L1_attn_in['A_log'], 'L1_attn_norm_w': _L1_attn_in['norm_w'], 'L1_attn_W_o': _L1_attn_in['W_o'], 'L1_xattn_Wq': _L1_xattn_in['Wq'], 'L1_xattn_bq': _L1_xattn_in['bq'], 'L1_xattn_Wk': _L1_xattn_in['Wk'], 'L1_xattn_bk': _L1_xattn_in['bk'], 'L1_xattn_Wv': _L1_xattn_in['Wv'], 'L1_xattn_bv': _L1_xattn_in['bv'], 'L1_xattn_Wo': _L1_xattn_in['Wo'], 'L1_xattn_bo': _L1_xattn_in['bo'], 'L1_ffn_gate_W': _L1_ffn_in['gate_W'], 'L1_ffn_gate_b': _L1_ffn_in['gate_b'], 'L1_ffn_W1': _L1_ffn_in['W1'], 'L1_ffn_b1': _L1_ffn_in['b1'], 'L1_ffn_W2': _L1_ffn_in['W2'], 'L1_ffn_b2': _L1_ffn_in['b2'], 'L2_attn_in_proj_w': _L2_attn_in['in_proj_w'], 'L2_attn_conv_w': _L2_attn_in['conv_w'], 'L2_attn_conv_b': _L2_attn_in['conv_b'], 'L2_attn_x_proj_w': _L2_attn_in['x_proj_w'], 'L2_attn_dt_proj_w': _L2_attn_in['dt_proj_w'], 'L2_attn_dt_proj_b': _L2_attn_in['dt_proj_b'], 'L2_attn_dt_ln_w': _L2_attn_in['dt_ln_w'], 'L2_attn_b_ln_w': _L2_attn_in['b_ln_w'], 'L2_attn_c_ln_w': _L2_attn_in['c_ln_w'], 'L2_attn_A_log': _L2_attn_in['A_log'], 'L2_attn_D': _L2_attn_in['D'], 'L2_attn_out_proj_w': _L2_attn_in['out_proj_w'], 'L2_ffn_Wr': _L2_ffn_in['Wr'], 'L2_ffn_W1': _L2_ffn_in['W1'], 'L2_ffn_b1': _L2_ffn_in['b1'], 'L2_ffn_W2': _L2_ffn_in['W2'], 'L2_ffn_b2': _L2_ffn_in['b2'], 'L3_attn_w_attn': _L3_attn_in['w_attn'], 'L3_attn_w_proj': _L3_attn_in['w_proj'], 'L3_xattn_W_diff': _L3_xattn_in['W_diff'], 'L3_xattn_b_diff': _L3_xattn_in['b_diff'], 'L3_xattn_ln_g': _L3_xattn_in['ln_g'], 'L3_xattn_ln_b': _L3_xattn_in['ln_b'], 'L3_xattn_W1': _L3_xattn_in['W1'], 'L3_xattn_b1': _L3_xattn_in['b1'], 'L3_xattn_W2': _L3_xattn_in['W2'], 'L3_xattn_b2': _L3_xattn_in['b2'], 'L3_ffn_ln1_scale': _L3_ffn_in['ln1_scale'], 'L3_ffn_ln1_bias': _L3_ffn_in['ln1_bias'], 'L3_ffn_w_qkv': _L3_ffn_in['w_qkv'], 'L3_ffn_b_qkv': _L3_ffn_in['b_qkv'], 'L3_ffn_w_attnproj': _L3_ffn_in['w_attnproj'], 'L3_ffn_b_attnproj': _L3_ffn_in['b_attnproj'], 'L3_ffn_ln2_scale': _L3_ffn_in['ln2_scale'], 'L3_ffn_ln2_bias': _L3_ffn_in['ln2_bias'], 'L3_ffn_w_gate': _L3_ffn_in['w_gate'], 'L3_ffn_b_gate': _L3_ffn_in['b_gate'], 'L3_ffn_w_fc': _L3_ffn_in['w_fc'], 'L3_ffn_b_fc': _L3_ffn_in['b_fc'], 'L3_ffn_w_fcproj': _L3_ffn_in['w_fcproj'], 'L3_ffn_b_fcproj': _L3_ffn_in['b_fcproj']}

def reference(x, ctx_1024, mask_Bx1xSxS2_ik1, L0_attn_Wq, L0_attn_bq, L0_attn_Wk, L0_attn_bk, L0_attn_Wv, L0_attn_bv, L0_attn_Wo, L0_attn_bo, L0_ffn_w_gate, L0_ffn_w_up, L0_ffn_w_down, L1_attn_W_in, L1_attn_W_ba, L1_attn_conv_w, L1_attn_dt_bias, L1_attn_A_log, L1_attn_norm_w, L1_attn_W_o, L1_xattn_Wq, L1_xattn_bq, L1_xattn_Wk, L1_xattn_bk, L1_xattn_Wv, L1_xattn_bv, L1_xattn_Wo, L1_xattn_bo, L1_ffn_gate_W, L1_ffn_gate_b, L1_ffn_W1, L1_ffn_b1, L1_ffn_W2, L1_ffn_b2, L2_attn_in_proj_w, L2_attn_conv_w, L2_attn_conv_b, L2_attn_x_proj_w, L2_attn_dt_proj_w, L2_attn_dt_proj_b, L2_attn_dt_ln_w, L2_attn_b_ln_w, L2_attn_c_ln_w, L2_attn_A_log, L2_attn_D, L2_attn_out_proj_w, L2_ffn_Wr, L2_ffn_W1, L2_ffn_b1, L2_ffn_W2, L2_ffn_b2, L3_attn_w_attn, L3_attn_w_proj, L3_xattn_W_diff, L3_xattn_b_diff, L3_xattn_ln_g, L3_xattn_ln_b, L3_xattn_W1, L3_xattn_b1, L3_xattn_W2, L3_xattn_b2, L3_ffn_ln1_scale, L3_ffn_ln1_bias, L3_ffn_w_qkv, L3_ffn_b_qkv, L3_ffn_w_attnproj, L3_ffn_b_attnproj, L3_ffn_ln2_scale, L3_ffn_ln2_bias, L3_ffn_w_gate, L3_ffn_b_gate, L3_ffn_w_fc, L3_ffn_b_fc, L3_ffn_w_fcproj, L3_ffn_b_fcproj):
    import jax
    import jax.numpy as jnp

    def _L0_attn_ref(x, Wq, bq, Wk, bk, Wv, bv, Wo, bo):
        import jax, jax.numpy as jnp
        import numpy as np
        B, T, C = (4, 512, 128)
        H = 16
        D = C // H
        W_SCALE = 0.02
        Bx, Tx, Cx = x.shape
        q = (x @ Wq.T + bq).reshape(Bx, Tx, H, D)
        k = (x @ Wk.T + bk).reshape(Bx, Tx, H, D)
        v = (x @ Wv.T + bv).reshape(Bx, Tx, H, D)
        q = jax.nn.elu(q) + 1.0
        k = jax.nn.elu(k) + 1.0
        kv = jnp.einsum('bthd,bthe->bhde', k, v)
        denom = jnp.einsum('bthd,bhd->bth', q, k.sum(axis=1))
        num = jnp.einsum('bthd,bhde->bthe', q, kv)
        out = num / jnp.clip(denom, 1e-06, None)[..., None]
        out = out.reshape(Bx, Tx, Cx)
        return out @ Wo.T + bo

    def _L0_xattn_ref(q, k, v):
        import jax, jax.numpy as jnp
        import numpy as np
        DECAY = 0.9
        kv = jnp.swapaxes(k * v, 0, 1)

        def step(r, kv_t):
            r = DECAY * r + kv_t
            return (r, r)
        r0 = jnp.zeros(q.shape[:1] + q.shape[2:], dtype=q.dtype)
        _, rs = jax.lax.scan(step, r0, kv)
        return q * jnp.swapaxes(rs, 0, 1)

    def _L0_ffn_ref(x, w_gate, w_up, w_down):
        import jax, jax.numpy as jnp
        import numpy as np
        BLOCK = 16
        _GRID = jnp.array([0.0, 0.5, 1.0, 1.5, 2.0, 3.0, 4.0, 6.0], dtype=jnp.float32)
        _MID = jnp.array([0.25, 0.75, 1.25, 1.75, 2.5, 3.5, 5.0], dtype=jnp.float32)

        def fp4_quant_dequant(x):
            shape = x.shape
            xb = x.reshape(shape[:-1] + (shape[-1] // BLOCK, BLOCK))
            scale = jnp.max(jnp.abs(xb), axis=-1, keepdims=True) / 6.0
            scale = jnp.maximum(scale, jnp.float32(1e-12))
            xn = xb / scale
            idx = jnp.searchsorted(_MID, jnp.abs(xn))
            q = _GRID[idx] * jnp.sign(xn) * scale
            return q.reshape(shape)

        def fp4_linear(x, w):
            xq = fp4_quant_dequant(x)
            wq = fp4_quant_dequant(w)
            return jnp.einsum('bsk,nk->bsn', xq, wq)
        gate = fp4_linear(x, w_gate)
        y = fp4_linear(x, w_up)
        h = jax.nn.silu(gate) * y
        return fp4_linear(h, w_down)

    def _L1_attn_ref(x, W_in, W_ba, conv_w, dt_bias, A_log, norm_w, W_o):
        import jax, jax.numpy as jnp
        import numpy as np
        B, T, D = (2, 512, 128)
        H, HD = (16, 64)
        KV = H * HD

        def _l2norm(t, eps=1e-06):
            return t * jax.lax.rsqrt(jnp.sum(t * t, axis=-1, keepdims=True) + eps)
        Bb, Tt, _ = x.shape
        qkvz = x @ W_in
        q, k, v, z = jnp.split(qkvz, 4, axis=-1)
        b, a = jnp.split(x @ W_ba, 2, axis=-1)
        qkv = jnp.concatenate([q, k, v], axis=-1).transpose(0, 2, 1)
        qkv = jax.lax.conv_general_dilated(qkv, conv_w, window_strides=(1,), padding=[(3, 0)], feature_group_count=3 * KV, dimension_numbers=('NCH', 'OIH', 'NCH'))
        qkv = jax.nn.silu(qkv).transpose(0, 2, 1)
        q, k, v = jnp.split(qkv, 3, axis=-1)
        rs = lambda t: t.reshape(Bb, Tt, H, HD)
        q, k, v, z = (rs(q), rs(k), rs(v), rs(z))
        beta = jax.nn.sigmoid(b)
        A = jnp.exp(jnp.maximum(A_log, -2.3))
        g = -A * jax.nn.softplus(a + dt_bias)
        q = _l2norm(q) * HD ** (-0.5)
        k = _l2norm(k)
        tm = lambda t: jnp.swapaxes(t, 0, 1)

        def step(S, inp):
            qt, kt, vt, gt, bt = inp
            S = S * jnp.exp(gt)[..., None, None]
            pred = jnp.einsum('bhk,bhkv->bhv', kt, S)
            S = S + jnp.einsum('bhk,bhv->bhkv', kt, (vt - pred) * bt[..., None])
            o = jnp.einsum('bhk,bhkv->bhv', qt, S)
            return (S, o)
        S0 = jnp.zeros((Bb, H, HD, HD), jnp.float32)
        _, y = jax.lax.scan(step, S0, (tm(q), tm(k), tm(v), tm(g), tm(beta)))
        y = jnp.swapaxes(y, 0, 1)
        y = y * jax.lax.rsqrt(jnp.mean(y * y, axis=-1, keepdims=True) + 1e-06)
        y = norm_w * y * jax.nn.silu(z)
        return y.reshape(Bb, Tt, KV) @ W_o

    def _L1_xattn_ref(query, key, value, mask, Wq, bq, Wk, bk, Wv, bv, Wo, bo):
        import jax, jax.numpy as jnp
        import numpy as np
        EMBED_DIM = 128
        NUM_HEADS = 16
        HEAD_DIM = EMBED_DIM // NUM_HEADS
        SCALE = HEAD_DIM ** (-0.5)
        B, NQ, NK = (2, 256, 256)
        b, nq, c = query.shape
        nk = key.shape[1]
        q = (query @ Wq + bq).reshape(b, nq, NUM_HEADS, HEAD_DIM).transpose(0, 2, 1, 3)
        k = (key @ Wk + bk).reshape(b, nk, NUM_HEADS, HEAD_DIM).transpose(0, 2, 1, 3)
        v = (value @ Wv + bv).reshape(b, nk, NUM_HEADS, HEAD_DIM).transpose(0, 2, 1, 3)
        attn = jnp.einsum('bhqd,bhkd->bhqk', q, k) * SCALE
        attn = jnp.where(mask == 0, -jnp.inf, attn)
        attn = jax.nn.softmax(attn, axis=-1)
        x = jnp.einsum('bhqk,bhkd->bhqd', attn, v)
        x = x.transpose(0, 2, 1, 3).reshape(b, nq, c)
        return x @ Wo + bo

    def _L1_ffn_ref(x, gate_W, gate_b, W1, b1, W2, b2):
        import jax, jax.numpy as jnp
        import numpy as np
        B, T, D, DFF, E = (4, 256, 128, 512, 8)
        b, t, d = x.shape
        num_experts = gate_W.shape[-1]
        logits = jnp.einsum('btd,de->bte', x, gate_W) + gate_b
        top1 = jnp.argmax(logits, axis=-1).reshape(-1)
        flat_x = x.reshape(b * t, d)
        out = jnp.zeros_like(flat_x)
        for e in range(num_experts):
            mask = (top1 == e).astype(x.dtype)[:, None]
            h = jax.nn.gelu(flat_x * mask @ W1[e] + b1[e], approximate=False)
            out = out + (h @ W2[e] + b2[e]) * mask
        return out.reshape(b, t, d)

    def _L2_attn_ref(hidden_states, in_proj_w, conv_w, conv_b, x_proj_w, dt_proj_w, dt_proj_b, dt_ln_w, b_ln_w, c_ln_w, A_log, D, out_proj_w):
        import jax, jax.numpy as jnp
        import numpy as np
        from jax import lax
        H = 128
        EXPAND = 2
        I = EXPAND * H
        N = 16
        K = 4
        R = 64
        EPS = 1e-06
        B_SZ, L = (2, 128)

        def rmsnorm(x, w):
            v = jnp.mean(x.astype(jnp.float32) ** 2, axis=-1, keepdims=True)
            return w * (x * jax.lax.rsqrt(v + EPS)).astype(x.dtype)
        b, l, _ = hidden_states.shape
        proj = hidden_states @ in_proj_w.T
        hs, gate = (proj[..., :I], proj[..., I:])
        x = jnp.transpose(hs, (0, 2, 1))
        x = lax.conv_general_dilated(x, conv_w, (1,), [(1, 2)], feature_group_count=I, dimension_numbers=('NCH', 'OIH', 'NCH'))
        x = x + conv_b[None, :, None]
        u = jax.nn.silu(jnp.transpose(x, (0, 2, 1)))
        x_dbl = u @ x_proj_w.T
        dt = rmsnorm(x_dbl[..., :R], dt_ln_w)
        Bm = rmsnorm(x_dbl[..., R:R + N], b_ln_w)
        Cm = rmsnorm(x_dbl[..., R + N:], c_ln_w)
        dt = jax.nn.softplus(dt @ dt_proj_w.T + dt_proj_b)
        A = -jnp.exp(A_log)
        dA = jnp.exp(dt[..., None] * A)
        dBu = (dt * u)[..., None] * Bm[:, :, None, :]

        def step(h, inp):
            dA_t, dBu_t = inp
            h = dA_t * h + dBu_t
            return (h, h)
        h0 = jnp.zeros((b, I, N), jnp.float32)
        _, h_seq = lax.scan(step, h0, (jnp.transpose(dA, (1, 0, 2, 3)), jnp.transpose(dBu, (1, 0, 2, 3))))
        y = jnp.einsum('lbin,bln->bli', h_seq, Cm)
        y = y + u * D
        y = y * jax.nn.silu(gate)
        return y @ out_proj_w.T

    def _L2_xattn_ref(query, value):
        import jax, jax.numpy as jnp
        import numpy as np
        B, SQ, SV, D = (8, 256, 256, 128)
        scores = jnp.einsum('bqd,bkd->bqk', query, value)
        distribution = jax.nn.softmax(scores, axis=-1)
        attention = jnp.einsum('bqk,bkd->bqd', distribution, value)
        return attention

    def _L2_ffn_ref(x, Wr, W1, b1, W2, b2):
        import jax, jax.numpy as jnp
        import numpy as np
        from math import ceil
        CAPACITY_FACTOR = 2.0
        MIN_CAPACITY = 4
        B, S, D = x.shape
        E = Wr.shape[1]
        N = B * S
        k = max(MIN_CAPACITY, ceil(N * CAPACITY_FACTOR / E))
        xt = x.reshape(N, D)
        scores = jax.nn.softmax(xt @ Wr, axis=-1)
        G, idx = jax.lax.top_k(scores.T, k)
        X_in = xt[idx]
        h = jax.nn.gelu(jnp.einsum('ekd,edh->ekh', X_in, W1) + b1[:, None, :], approximate=False)
        X_e = jnp.einsum('ekh,ehd->ekd', h, W2) + b2[:, None, :]
        contrib = (G[..., None] * X_e).reshape(E * k, D)
        out = jnp.zeros((N, D), dtype=x.dtype).at[idx.reshape(-1)].add(contrib)
        return out.reshape(B, S, D)

    def _L3_attn_ref(x, w_attn, w_proj):
        import jax, jax.numpy as jnp
        import numpy as np
        N_HEAD = 16
        EPS = 1e-06

        def _linear_attention(q, k, v):
            B, H, D = (q.shape[1], q.shape[2], q.shape[3])

            def step(carry, qkv_t):
                S, z = carry
                qt, kt, vt = qkv_t
                S = S + kt[..., :, None] * vt[..., None, :]
                z = z + kt
                num = jnp.einsum('bhi,bhij->bhj', qt, S)
                den = jnp.sum(qt * z, axis=-1, keepdims=True)
                return ((S, z), num / (den + EPS))
            S0 = jnp.zeros((B, H, D, D), q.dtype)
            z0 = jnp.zeros((B, H, D), q.dtype)
            _, y = jax.lax.scan(step, (S0, z0), (q, k, v))
            return y
        B, T, C = x.shape
        H = N_HEAD
        D = C // H
        qkv = x @ w_attn
        q, k, v = jnp.split(qkv, 3, axis=-1)

        def to_tbhd(a):
            return a.reshape(B, T, H, D).transpose(1, 0, 2, 3)
        q = jax.nn.elu(to_tbhd(q)) + 1.0
        k = jax.nn.elu(to_tbhd(k)) + 1.0
        v = to_tbhd(v)
        y = _linear_attention(q, k, v)
        y = y.transpose(1, 0, 2, 3).reshape(B, T, C)
        return y @ w_proj

    def _L3_xattn_ref(q, k, v, W_diff, b_diff, ln_g, ln_b, W1, b1, W2, b2):
        import jax, jax.numpy as jnp
        import numpy as np
        EPS = 1e-08
        LN_EPS = 1e-05

        def _layernorm(x, g, b):
            mu = jnp.mean(x, axis=-1, keepdims=True)
            var = jnp.var(x, axis=-1, keepdims=True)
            return (x - mu) * jax.lax.rsqrt(var + LN_EPS) * g + b

        def _prob(x):
            x = jnp.tanh(x) * 0.499 + 0.5
            return jnp.clip(x / (jnp.sum(x, axis=-1, keepdims=True) + EPS), EPS)
        D = q.shape[-1]
        q_prob = _prob(q)
        k_prob = _prob(k)
        log_ratio = jnp.log(q_prob) - jnp.log(k_prob)
        sid = jnp.einsum('bnd,bmd->bnm', q_prob - k_prob, log_ratio)
        sid_sim = -sid
        attn = jax.nn.softmax(sid_sim / D ** 0.5, axis=-1)
        attn_feat = jnp.einsum('bnm,bmd->bnd', attn, v)
        f_diff = (v - attn_feat) @ W_diff.T + b_diff + q
        h = _layernorm(f_diff, ln_g, ln_b)
        mlp = jax.nn.gelu(h @ W1.T + b1, approximate=False) @ W2.T + b2
        out = mlp + f_diff
        return _layernorm(out, ln_g, ln_b)

    def _L3_ffn_ref(x, ln1_scale, ln1_bias, w_qkv, b_qkv, w_attnproj, b_attnproj, ln2_scale, ln2_bias, w_gate, b_gate, w_fc, b_fc, w_fcproj, b_fcproj):
        import jax, jax.numpy as jnp
        import numpy as np
        B, T, N = (2, 256, 128)
        H = 16
        E = 8
        K = 2
        FF = 4 * N
        EPS = 1e-05
        SCALE = 1.0

        def _layernorm(x, scale, bias):
            mu = x.mean(-1, keepdims=True)
            var = ((x - mu) ** 2).mean(-1, keepdims=True)
            return (x - mu) * jax.lax.rsqrt(var + EPS) * scale + bias

        def _attention(x, w_qkv, b_qkv, w_proj, b_proj):
            b, t, n = x.shape
            qkv = x @ w_qkv + b_qkv
            q, k, v = jnp.split(qkv, 3, axis=2)
            hd = n // H
            q = q.reshape(b, t, H, hd).transpose(0, 2, 1, 3)
            k = k.reshape(b, t, H, hd).transpose(0, 2, 1, 3)
            v = v.reshape(b, t, H, hd).transpose(0, 2, 1, 3)
            att = jnp.einsum('bhqd,bhkd->bhqk', q, k) / hd ** 0.5
            mask = jnp.tril(jnp.ones((1, 1, t, t), bool))
            att = jnp.where(mask, att, jnp.finfo(jnp.float32).min)
            att = jax.nn.softmax(att, axis=-1)
            y = jnp.einsum('bhqk,bhkd->bhqd', att, v)
            y = y.transpose(0, 2, 1, 3).reshape(b, t, n)
            return y @ w_proj + b_proj

        def _moe(x, w_gate, b_gate, w_fc, b_fc, w_fcproj, b_fcproj):
            b, t, n = x.shape
            xf = x.reshape(-1, n)
            bt = xf.shape[0]
            logits = xf @ w_gate + b_gate
            probs = jax.nn.softmax(logits, axis=-1)
            top_p, top_i = jax.lax.top_k(probs, K)
            out = jnp.zeros((bt, n), xf.dtype)
            expert_mask = jnp.transpose(jax.nn.one_hot(top_i, E), (2, 1, 0))
            rows = jnp.arange(bt)
            for e in range(E):
                active = expert_mask[e]
                mask = active.any(axis=0)
                cumsum = jnp.cumsum(mask) - 1
                indices = jnp.where(mask, cumsum, -1)
                sel = jnp.where(mask[:, None], xf, 0.0)
                h = jax.nn.gelu(sel @ w_fc[e] + b_fc[e], approximate=True)
                eo = h @ w_fcproj[e] + b_fcproj[e]
                rp = jnp.where(mask[:, None], top_p[rows, jnp.argmax(active, axis=0)][:, None], 0.0)
                out = out.at[indices].add(eo * rp)
            return out.reshape(b, t, n)
        x = x + SCALE * _attention(_layernorm(x, ln1_scale, ln1_bias), w_qkv, b_qkv, w_attnproj, b_attnproj)
        x = x + SCALE * _moe(_layernorm(x, ln2_scale, ln2_bias), w_gate, b_gate, w_fc, b_fc, w_fcproj, b_fcproj)
        return x
    x = x + _L0_attn_ref(_layernorm(x, axis=-1), L0_attn_Wq, L0_attn_bq, L0_attn_Wk, L0_attn_bk, L0_attn_Wv, L0_attn_bv, L0_attn_Wo, L0_attn_bo)
    x = x + _L0_xattn_ref(_layernorm(x, axis=-1), ctx_1024, ctx_1024)
    x = x + _L0_ffn_ref(_layernorm(x, axis=-1), L0_ffn_w_gate, L0_ffn_w_up, L0_ffn_w_down)
    x = x + _L1_attn_ref(_layernorm(x, axis=-1), L1_attn_W_in, L1_attn_W_ba, L1_attn_conv_w, L1_attn_dt_bias, L1_attn_A_log, L1_attn_norm_w, L1_attn_W_o)
    x = x + _L1_xattn_ref(_layernorm(x, axis=-1), ctx_1024, ctx_1024, mask_Bx1xSxS2_ik1, L1_xattn_Wq, L1_xattn_bq, L1_xattn_Wk, L1_xattn_bk, L1_xattn_Wv, L1_xattn_bv, L1_xattn_Wo, L1_xattn_bo)
    x = x + _L1_ffn_ref(_layernorm(x, axis=-1), L1_ffn_gate_W, L1_ffn_gate_b, L1_ffn_W1, L1_ffn_b1, L1_ffn_W2, L1_ffn_b2)
    x = x + _L2_attn_ref(_layernorm(x, axis=-1), L2_attn_in_proj_w, L2_attn_conv_w, L2_attn_conv_b, L2_attn_x_proj_w, L2_attn_dt_proj_w, L2_attn_dt_proj_b, L2_attn_dt_ln_w, L2_attn_b_ln_w, L2_attn_c_ln_w, L2_attn_A_log, L2_attn_D, L2_attn_out_proj_w)
    x = x + _L2_xattn_ref(_layernorm(x, axis=-1), ctx_1024)
    x = x + _L2_ffn_ref(_layernorm(x, axis=-1), L2_ffn_Wr, L2_ffn_W1, L2_ffn_b1, L2_ffn_W2, L2_ffn_b2)
    x = x + _L3_attn_ref(_layernorm(x, axis=-1), L3_attn_w_attn, L3_attn_w_proj)
    x = x + _L3_xattn_ref(_layernorm(x, axis=-1), ctx_1024, ctx_1024, L3_xattn_W_diff, L3_xattn_b_diff, L3_xattn_ln_g, L3_xattn_ln_b, L3_xattn_W1, L3_xattn_b1, L3_xattn_W2, L3_xattn_b2)
    x = x + _L3_ffn_ref(_layernorm(x, axis=-1), L3_ffn_ln1_scale, L3_ffn_ln1_bias, L3_ffn_w_qkv, L3_ffn_b_qkv, L3_ffn_w_attnproj, L3_ffn_b_attnproj, L3_ffn_ln2_scale, L3_ffn_ln2_bias, L3_ffn_w_gate, L3_ffn_b_gate, L3_ffn_w_fc, L3_ffn_b_fc, L3_ffn_w_fcproj, L3_ffn_b_fcproj)
    return x

_drawn_inputs = setup_inputs


def setup_inputs(seed=0):
    import zlib

    import numpy as np

    out = dict(_drawn_inputs(seed))
    spreads = {'L0_attn_bq': (0.0, 0.8),
     'L0_attn_bk': (0.0, 0.8),
     'L0_attn_bv': (0.0, 0.1),
     'L0_attn_bo': (0.0, 0.1),
     'L1_attn_dt_bias': (1.0, 0.6),
     'L1_attn_norm_w': (1.0, 0.596),
     'L1_xattn_bq': (0.0, 0.312),
     'L1_xattn_bk': (0.0, 2.0),
     'L1_xattn_bv': (0.0, 0.277),
     'L1_xattn_bo': (0.0, 0.304),
     'L1_ffn_gate_b': (0.0, 0.1),
     'L1_ffn_b1': (0.0, 0.32),
     'L1_ffn_b2': (0.0, 0.299),
     'L2_attn_conv_b': (0.0, 0.8),
     'L2_attn_dt_ln_w': (1.0, 0.6),
     'L2_attn_b_ln_w': (1.0, 0.6),
     'L2_attn_c_ln_w': (1.0, 0.6),
     'L2_attn_D': (1.0, 0.6),
     'L2_ffn_b1': (0.0, 0.329),
     'L2_ffn_b2': (0.0, 0.373),
     'L3_xattn_b_diff': (0.0, 0.295),
     'L3_xattn_ln_g': (1.0, 0.55),
     'L3_xattn_ln_b': (0.0, 0.288),
     'L3_xattn_b1': (0.0, 0.399),
     'L3_xattn_b2': (0.0, 0.302),
     'L3_ffn_ln1_scale': (1.0, 0.569),
     'L3_ffn_ln1_bias': (0.0, 0.28),
     'L3_ffn_b_qkv': (0.0, 0.278),
     'L3_ffn_b_attnproj': (0.0, 0.276),
     'L3_ffn_ln2_scale': (1.0, 0.6),
     'L3_ffn_ln2_bias': (0.0, 0.285),
     'L3_ffn_b_gate': (0.0, 0.288),
     'L3_ffn_b_fc': (0.0, 2.0),
     'L3_ffn_b_fcproj': (0.0, 0.8)}
    factors = {'L0_attn_Wq': 8.0,
     'L0_attn_Wk': 4.835,
     'L0_attn_Wv': 3.131,
     'L0_ffn_w_gate': 3.562,
     'L0_ffn_w_up': 3.807,
     'L0_ffn_w_down': 4.294,
     'L1_attn_W_ba': 2.796,
     'L1_attn_A_log': 2.763,
     'L2_attn_in_proj_w': 7.5,
     'L2_attn_conv_w': 8.0,
     'L2_attn_x_proj_w': 8.0,
     'L2_attn_dt_proj_w': 8.0,
     'L2_attn_dt_proj_b': 8.0,
     'L2_attn_A_log': 8.0,
     'L2_attn_out_proj_w': 8.0,
     'L3_attn_w_attn': 3.488,
     'L3_attn_w_proj': 3.234,
     'L3_xattn_W1': 3.255,
     'L3_xattn_W2': 2.997,
     'L3_ffn_w_gate': 2.756,
     'L3_ffn_w_fc': 2.843}
    for name, (base, spread) in spreads.items():
        noise = np.random.default_rng([zlib.crc32(name.encode()), seed]).standard_normal(out[name].shape)
        drawn = base * np.exp(spread * noise) if base else spread * noise
        out[name] = jnp.asarray(drawn.astype(out[name].dtype))
    for name, factor in factors.items():
        out[name] = (out[name] * factor).astype(out[name].dtype)
    return out
```

```python
from contextlib import ExitStack

import numpy as np
import concourse.bass as bass
from concourse import mybir

ALU = mybir.AluOpType
ACT = mybir.ActivationFunctionType
AX = mybir.AxisListType
F32 = mybir.dt.float32
I32 = mybir.dt.int32
U32 = mybir.dt.uint32

NB, T, D = 32, 128, 128
GB = 4
NG = NB // GB
GT = GB * T
H, HD = 16, 8
LN_EPS = 1e-5


class Chain:

    def __init__(self, sem):
        self.sem, self.base, self.n = sem, 0, 0

    def __call__(self, eng, ins):
        self.n += 1
        ins.then_inc(self.sem, 1)
        eng.wait_ge(self.sem, self.base + self.n)

    def turn(self, base, turn, per_turn):
        self.base, self.n = base + turn * per_turn, 0

    def turned(self, base, turns, per_turn):
        assert self.n == per_turn, (self.n, per_turn)
        self.base, self.n = base + turns * per_turn, 0


class Stage:

    def __init__(self, nc, name):
        self.nc, self.name, self.sems = nc, name, []
        self.stack = ExitStack()

    def __enter__(self):
        return self

    def sb(self, name, shape, dt=F32):
        return self.stack.enter_context(self.nc.sbuf_tensor(f"{self.name}_{name}", shape, dt))

    def sem(self, name):
        s = self.nc.alloc_semaphore(f"{self.name}_{name}")
        self.sems.append(s)
        return s

    def __exit__(self, *e):
        if e[0] is None:
            self.nc.clear_and_free_semaphores(self.sems)
            self.nc.all_engine_barrier()
            self.stack.close()


def over(ap, *shape):
    return ap.to_broadcast(list(shape))


def load_stage(nc, m, a):
    with Stage(nc, "load") as st:
        loaded, turned, copied = st.sem("loaded"), st.sem("turned"), st.sem("copied")
        with nc.Block() as block:
            @block.sync
            def _(sp):
                sp.dma_start(m.ident[:], a["c_ident"]).then_inc(loaded, 16)
                sp.dma_start(m.x[:], a["x"].rearrange("b t d -> t b d")).then_inc(loaded, 16)
                sp.dma_start(m.ones[:], a["c_ones"]).then_inc(loaded, 16)
                sp.dma_start(m.causal[:], a["c_causal"]).then_inc(loaded, 16)
                sp.dma_start(m.heads[:], a["c_heads"]).then_inc(loaded, 16)
                sp.dma_start(m.ctx[:], a["ctx_1024"].rearrange("b t d -> t b d")).then_inc(loaded, 16)

            @block.tensor
            def _(pe):
                pe.wait_ge(loaded, 96)
                for g in range(NG):
                    for j in range(GB):
                        ins = nc.tensor.transpose(m.ps[:, g, j * T:(j + 1) * T], m.ctx[:, GB * g + j, :], m.ident[:])
                    ins.then_inc(turned, 1)

            @block.scalar
            def _(act):
                for g in range(NG):
                    act.wait_ge(turned, g + 1)
                    nc.scalar.copy(m.ctxt[:, g * GT:(g + 1) * GT], m.ps[:, g, :]).then_inc(copied, 1)
                act.wait_ge(copied, NG)


def norm_stage(nc, m, name, transposed=True, src=None, affine=None):
    src = m.x if src is None else src
    with Stage(nc, name) as st:
        stat = st.sb("stat", [128, 4, NB])
        sq = st.sb("sq", [128, NB, D])
        chain = Chain(st.sem("dve_order"))
        centred, squared = st.sem("centred"), st.sem("squared")
        var_ready, std_ready = st.sem("var_ready"), st.sem("std_ready")
        normed, turned, copied = st.sem("normed"), st.sem("turned"), st.sem("copied")
        loaded = st.sem("loaded")
        coef = st.sb("coef", [128, 2, D]) if affine else None
        with nc.Block() as block:
            if affine:
                @block.sync
                def _(sp):
                    for i in range(2):
                        sp.dma_start(coef[:, i, :], over(affine[i].unsqueeze(0), 128, D)).then_inc(loaded, 16)

            @block.vector
            def _(dve):
                chain(dve, nc.vector.tensor_reduce(stat[:, 0, :], src[:], AX.X, ALU.add))
                chain(dve, nc.vector.tensor_scalar(stat[:, 1, :], stat[:, 0, :], 1.0 / D, None, ALU.mult))
                nc.vector.tensor_tensor(m.xn[:], src[:], over(stat[:, 1, :].unsqueeze(2), 128, NB, D),
                                        ALU.subtract).then_inc(centred, 1)
                dve.wait_ge(squared, 1)
                chain(dve, nc.vector.tensor_reduce(stat[:, 2, :], sq[:], AX.X, ALU.add))
                nc.vector.tensor_scalar(stat[:, 3, :], stat[:, 2, :], 1.0 / D, LN_EPS, ALU.mult,
                                        ALU.add).then_inc(var_ready, 1)
                dve.wait_ge(std_ready, 1)
                chain(dve, nc.vector.reciprocal(stat[:, 1, :], stat[:, 0, :]))
                chain(dve, nc.vector.tensor_tensor(stat[:, 2, :], stat[:, 3, :], stat[:, 1, :], ALU.mult))
                chain(dve, nc.vector.tensor_tensor(stat[:, 2, :], stat[:, 2, :], stat[:, 1, :], ALU.mult))
                chain(dve, nc.vector.tensor_scalar(stat[:, 2, :], stat[:, 2, :], -0.5, 0.5, ALU.mult, ALU.add))
                chain(dve, nc.vector.tensor_tensor(stat[:, 2, :], stat[:, 2, :], stat[:, 1, :], ALU.mult))
                chain(dve, nc.vector.tensor_tensor(stat[:, 1, :], stat[:, 2, :], stat[:, 1, :], ALU.add))
                chain(dve, nc.vector.tensor_tensor(stat[:, 2, :], stat[:, 3, :], stat[:, 1, :], ALU.mult))
                chain(dve, nc.vector.tensor_tensor(stat[:, 2, :], stat[:, 2, :], stat[:, 1, :], ALU.mult))
                chain(dve, nc.vector.tensor_scalar(stat[:, 2, :], stat[:, 2, :], -0.5, 0.5, ALU.mult, ALU.add))
                chain(dve, nc.vector.tensor_tensor(stat[:, 2, :], stat[:, 2, :], stat[:, 1, :], ALU.mult))
                chain(dve, nc.vector.tensor_tensor(stat[:, 1, :], stat[:, 2, :], stat[:, 1, :], ALU.add))
                ins = nc.vector.tensor_tensor(m.xn[:], m.xn[:], over(stat[:, 1, :].unsqueeze(2), 128, NB, D), ALU.mult)
                if affine:
                    dve.wait_ge(loaded, 32)
                    chain(dve, ins)
                    chain(dve, nc.vector.tensor_tensor(m.xn[:], m.xn[:], over(coef[:, 0:1, :], 128, NB, D), ALU.mult))
                    ins = nc.vector.tensor_tensor(m.xn[:], m.xn[:], over(coef[:, 1:2, :], 128, NB, D), ALU.add)
                ins.then_inc(normed, 1)
                if transposed:
                    for g in range(1, NG, 2):
                        dve.wait_ge(turned, g + 1)
                        ins = nc.vector.tensor_copy(m.xt[:, g * GT:(g + 1) * GT], m.ps[:, g, :])
                    ins.then_inc(copied, 1)
                    dve.wait_ge(copied, 2)
                else:
                    dve.wait_ge(normed, 1)

            @block.scalar
            def _(act):
                act.wait_ge(centred, 1)
                nc.scalar.activation(sq[:], m.xn[:], ACT.Square).then_inc(squared, 1)
                act.wait_ge(var_ready, 1)
                nc.scalar.activation(stat[:, 0, :], stat[:, 3, :], ACT.Sqrt).then_inc(std_ready, 1)
                if transposed:
                    for g in range(0, NG, 2):
                        act.wait_ge(turned, g + 1)
                        ins = nc.scalar.copy(m.xt[:, g * GT:(g + 1) * GT], m.ps[:, g, :])
                    ins.then_inc(copied, 1)
                    act.wait_ge(copied, 2)

            @block.tensor
            def _(pe):
                if transposed:
                    pe.wait_ge(normed, 1)
                    for g in range(NG):
                        for j in range(GB):
                            ins = nc.tensor.transpose(m.ps[:, g, j * T:(j + 1) * T], m.xn[:, GB * g + j, :],
                                                      m.ident[:])
                        ins.then_inc(turned, 1)


def stage_groups(nc, xg, src, staged, taken, ready, n_ready):
    def program(pool):
        with nc.gpsimd.Fori(0, NG) as g:
            pool.wait_ge(taken, g)
            pool.wait_ge(ready, n_ready)
            nc.gpsimd.tensor_copy(xg[:], src[:, bass.ts(g, GT)]).then_inc(staged, 1)
    return program


def l0_attn_stage(nc, m, a):
    with Stage(nc, "l0a") as st:
        wq, wkv, wo = st.sb("wq", [128, D]), st.sb("wkv", [128, 2 * D]), st.sb("wo", [128, D])
        bq, bkv, bo = st.sb("bq", [1, D]), st.sb("bkv", [1, 2 * D]), st.sb("bo", [128, D])
        low, ex = st.sb("low", [128, 2, GT]), st.sb("ex", [128, 2, GT])
        qt, kk = st.sb("qt", [128, GT]), st.sb("kk", [128, GB, D])
        v1 = st.sb("v1", [128, GB, 2 * D])
        kv = st.sb("kv", [128, GB, 2 * D])
        den, rec, ot = st.sb("den", [128, GT]), st.sb("rec", [128, GT]), st.sb("ot", [128, GT])
        loaded, ones_set = st.sem("loaded"), st.sem("ones_set")
        xg, staged = st.sb("xg", [128, GT]), st.sem("staged")
        q_made, kv_made = st.sem("q_made"), st.sem("kv_made")
        q_low, k_low, q_exp, k_exp = st.sem("q_low"), st.sem("k_low"), st.sem("q_exp"), st.sem("k_exp")
        v_kept, features, states, states_kept = st.sem("v_kept"), st.sem("features"), st.sem("states"), st.sem("states_kept")
        read, read_kept, projected, added = st.sem("read"), st.sem("read_kept"), st.sem("projected"), st.sem("added")
        biased, chain = st.sem("biased"), Chain(st.sem("dve_order"))
        qp, kvp = m.ps[:, 0, :], m.ps[:, 1:3, :].rearrange("p a (b c) -> p (a b) c", c=2 * D)
        sp_ = m.ps[:, 3:5, :].rearrange("p a (b c) -> p (a b) c", c=2 * D)
        nump, denp, yp = m.ps[:, 5, :], m.ps[:, 6, :], m.ps[:, 7, :]
        with nc.Block() as block:
            @block.sync
            def _(sp):
                sp.dma_start(wq[:], a["L0_attn_WqT"]).then_inc(loaded, 16)
                sp.dma_start(wkv[:, 0:D], a["L0_attn_WkT"]).then_inc(loaded, 16)
                sp.dma_start(wkv[:, D:2 * D], a["L0_attn_WvT"]).then_inc(loaded, 16)
                sp.dma_start(wo[:], a["L0_attn_WoT"]).then_inc(loaded, 16)
                sp.dma_start(bq[:], a["L0_attn_bq"].unsqueeze(0)).then_inc(loaded, 16)
                sp.dma_start(bkv[:, 0:D], a["L0_attn_bk"].unsqueeze(0)).then_inc(loaded, 16)
                sp.dma_start(bkv[:, D:2 * D], a["L0_attn_bv"].unsqueeze(0)).then_inc(loaded, 16)
                sp.dma_start(bo[:], over(a["L0_attn_bo"].unsqueeze(0), 128, D)).then_inc(loaded, 16)

            block.gpsimd(stage_groups(nc, xg, m.xt, staged, kv_made, loaded, 8 * 16))

            @block.tensor
            def _(pe):
                pe.wait_ge(loaded, 8 * 16)
                with nc.tensor.Fori(0, NG) as g:
                    pe.wait_ge(features, g)
                    nc.tensor.matmul(qp, wq[:], m.xt[:, bass.ts(g, GT)], start=True, stop=False)
                    nc.tensor.matmul(qp, bq[:], m.ones[0:1, :], start=False, stop=True).then_inc(q_made, 1)
                    pe.wait_ge(staged, g + 1)
                    for j in range(GB):
                        nc.tensor.matmul(kvp[:, j, :], xg[:, j * T:(j + 1) * T], wkv[:],
                                         start=True, stop=False)
                        ins = nc.tensor.matmul(kvp[:, j, :], m.ones[0:1, 0:T], bkv[:], start=False, stop=True)
                    ins.then_inc(kv_made, 1)
                    pe.wait_ge(features, g + 1)
                    for j in range(GB):
                        ins = nc.tensor.matmul(sp_[:, j, :], kk[:, j, :], v1[:, j, :], start=True, stop=True)
                    ins.then_inc(states, 1)
                    pe.wait_ge(states_kept, g + 1)
                    for j in range(GB):
                        c = slice(j * T, (j + 1) * T)
                        nc.tensor.matmul(nump[:, c], kv[:, j, 0:D], qt[:, c], start=True, stop=True)
                        ins = nc.tensor.matmul(denp[:, c], kv[:, j, D:2 * D], qt[:, c], start=True, stop=True)
                    ins.then_inc(read, 1)
                    pe.wait_ge(read_kept, g + 1)
                    for j in range(GB):
                        c = slice(j * T, (j + 1) * T)
                        ins = nc.tensor.matmul(yp[:, c], ot[:, c], wo[:], start=True, stop=True)
                    ins.then_inc(projected, 1)

            @block.scalar
            def _(act):
                with nc.scalar.Fori(0, NG) as g:
                    act.wait_ge(q_low, g + 1)
                    nc.scalar.activation(ex[:, 0, :], low[:, 0, :], ACT.Exp).then_inc(q_exp, 1)
                    act.wait_ge(k_low, g + 1)
                    nc.scalar.activation(ex[:, 1, :], low[:, 1, :], ACT.Exp).then_inc(k_exp, 1)
                    act.wait_ge(kv_made, g + 1)
                    act.wait_ge(ones_set, 1)
                    nc.scalar.copy(v1[:, :, 0:D], kvp[:, :, D:2 * D]).then_inc(v_kept, 1)

            @block.vector
            def _(dve):
                nc.vector.memset(v1[:], 1.0).then_inc(ones_set, 1)
                dve.wait_ge(loaded, 8 * 16)
                nc.vector.tensor_tensor(m.x[:], m.x[:], over(bo[:].unsqueeze(1), 128, NB, D), ALU.add).then_inc(biased, 1)
                dve.wait_ge(biased, 1)
                with nc.vector.Fori(0, NG) as g:
                    chain.turn(0, g, 2)
                    dve.wait_ge(q_made, g + 1)
                    nc.vector.tensor_scalar(low[:, 0, :], qp, 0.0, None, ALU.min).then_inc(q_low, 1)
                    dve.wait_ge(kv_made, g + 1)
                    nc.vector.tensor_scalar(low[:, 1, :].rearrange("p (b c) -> p b c", c=D), kvp[:, :, 0:D], 0.0,
                                            None, ALU.min).then_inc(k_low, 1)
                    dve.wait_ge(q_exp, g + 1)
                    nc.vector.scalar_tensor_tensor(out=qt[:], in0=qp, scalar=0.0, in1=ex[:, 0, :], op0=ALU.max,
                                                   op1=ALU.add)
                    dve.wait_ge(k_exp, g + 1)
                    dve.wait_ge(v_kept, g + 1)
                    nc.vector.scalar_tensor_tensor(out=kk[:], in0=kvp[:, :, 0:D], scalar=0.0,
                                                   in1=ex[:, 1, :].rearrange("p (b c) -> p b c", c=D),
                                                   op0=ALU.max, op1=ALU.add).then_inc(features, 1)
                    dve.wait_ge(states, g + 1)
                    nc.vector.tensor_tensor(kv[:].rearrange("p b (s c) -> p (b s) c", s=2),
                                            sp_.rearrange("p b (s c) -> p (b s) c", s=2),
                                            over(m.heads[:].unsqueeze(1), 128, 2 * GB, D),
                                            ALU.mult).then_inc(states_kept, 1)
                    dve.wait_ge(read, g + 1)
                    chain(dve, nc.vector.tensor_scalar(den[:], denp, 1e-6, None, ALU.max))
                    chain(dve, nc.vector.reciprocal(rec[:], den[:]))
                    nc.vector.tensor_tensor(ot[:], nump, rec[:], ALU.mult).then_inc(read_kept, 1)
                    dve.wait_ge(projected, g + 1)
                    xs = m.x[:, bass.ts(g, GB), :]
                    nc.vector.tensor_tensor(xs, xs, yp.rearrange("p (b c) -> p b c", c=D),
                                            ALU.add).then_inc(added, 1)
                dve.wait_ge(added, NG)


def l0_xattn_stage(nc, m, a):
    with Stage(nc, "l0x") as st:
        decay = st.sb("decay", [128, GB, T])
        sq = st.sb("sq", [128, 2, GT])
        r = st.sb("r", [128, 2, GT])
        prod = st.sb("prod", [128, 2, GB, D])
        squared, turned, scaled, added = (st.sem(n) for n in ("squared", "turned", "scaled", "added"))
        set_, scanned = st.sem("set"), st.sem("scanned")
        with nc.Block() as block:
            @block.scalar
            def _(act):
                for g in range(NG):
                    if g >= 2:
                        act.wait_ge(scanned, g - 1)
                    nc.scalar.activation(sq[:, g % 2], m.ctxt[:, g * GT:(g + 1) * GT], ACT.Square).then_inc(squared, 1)

            @block.tensor
            def _(pe):
                for g in range(NG):
                    pe.wait_ge(scanned, g + 1)
                    for j in range(GB):
                        ins = nc.tensor.transpose(m.ps[:, g, j * T:(j + 1) * T], r[:, g % 2, j * T:(j + 1) * T], m.ident[:])
                    ins.then_inc(turned, 1)

            @block.vector
            def _(dve):
                nc.vector.memset(decay[:], 0.9).then_inc(set_, 1)
                dve.wait_ge(set_, 1)
                nc.vector.memset(decay[:, :, 0:1], 0.0).then_inc(set_, 1)
                dve.wait_ge(set_, 2)
                for g in range(NG + 1):
                    if g < NG:
                        dve.wait_ge(squared, g + 1)
                        if g >= 2:
                            dve.wait_ge(turned, g - 1)
                        nc.vector.tensor_tensor_scan(r[:, g % 2], decay[:].rearrange("p b t -> p (b t)"), sq[:, g % 2],
                                                     0.0, ALU.mult, ALU.add).then_inc(scanned, 1)
                    if g >= 1:
                        k = g - 1
                        dve.wait_ge(turned, k + 1)
                        s = slice(GB * k, GB * k + GB)
                        if k >= 2:
                            dve.wait_ge(added, k - 1)
                        nc.vector.tensor_tensor(prod[:, k % 2], m.ps[:, k, :].rearrange("p (b c) -> p b c", c=D),
                                                m.xn[:, s, :], ALU.mult).then_inc(scaled, 1)
                        dve.wait_ge(scaled, k + 1)
                        nc.vector.tensor_tensor(m.x[:, s, :], m.x[:, s, :], prod[:, k % 2], ALU.add).then_inc(added, 1)
                dve.wait_ge(added, NG)


def quantise(nc, dve, chain, x, mag, lev, sc, n_blocks):
    blocks = lambda t: t.rearrange("p (n k) -> p n k", k=16)
    wide = lambda t: over(t.unsqueeze(2), 128, n_blocks, 16)
    V = nc.vector
    chain(dve, V.tensor_reduce(sc[:, 0, :], blocks(x), AX.X, ALU.max, apply_absolute_value=True))
    chain(dve, V.tensor_scalar(sc[:, 0, :], sc[:, 0, :], 1.0 / 6.0, 1e-12, ALU.mult, ALU.max))
    chain(dve, V.reciprocal(sc[:, 1, :], sc[:, 0, :]))
    chain(dve, V.tensor_tensor(blocks(x), blocks(x), wide(sc[:, 1, :]), ALU.mult))
    chain(dve, V.scalar_tensor_tensor(out=mag, in0=x, scalar=-1.0, in1=x, op0=ALU.mult, op1=ALU.max))
    chain(dve, V.tensor_scalar(lev, mag, 5.0 * TIE, 4.0, ALU.is_gt, ALU.mult))
    for mid in (3.5, 3.5, 2.5, 2.5, 1.75, 1.25, 0.75, 0.25):
        chain(dve, V.scalar_tensor_tensor(out=lev, in0=mag, scalar=mid * TIE, in1=lev, op0=ALU.is_gt, op1=ALU.add))
    chain(dve, V.tensor_scalar(x, x, 0.0, 0.5, ALU.is_gt, ALU.subtract))
    chain(dve, V.tensor_tensor(x, x, lev, ALU.mult))
    chain(dve, V.tensor_tensor(blocks(x), blocks(x), wide(sc[:, 0, :]), ALU.mult))


QUANTISE_STEPS = 17
TIE = 1 + 2.0 ** -21
F0 = 352


def l0_ffn_stage(nc, m, a):
    KC = [(0, 128), (128, 128), (256, 96)]
    with Stage(nc, "l0f") as st:
        mag, lev = st.sb("mag", [128, NB * D]), st.sb("lev", [128, NB * D])
        sc = st.sb("sc", [128, 2, NB * D // 16])
        wraw = st.sb("wraw", [128, 7 * 128])
        wdraw = st.sb("wdraw", [128, F0])
        wgt, wut, wdt = st.sb("wgt", [128, 384]), st.sb("wut", [128, 384]), st.sb("wdt", [128, 3, D])
        hid, gate = st.sb("hid", [128, GB * F0]), st.sb("gate", [128, GB, F0])
        ht = st.sb("ht", [128, 3, GT])
        cleared, loaded, order = st.sem("cleared"), st.sem("loaded"), Chain(st.sem("dve_order"))
        w_quant, w_turned, w_kept = st.sem("w_quant"), st.sem("w_turned"), st.sem("w_kept")
        x_quant, x_turned, x_kept = st.sem("x_quant"), st.sem("x_turned"), st.sem("x_kept")
        up_made, silu_made, h_made, h_quant = (st.sem(n) for n in ("up_made", "silu_made", "h_made", "h_quant"))
        h_turned, h_kept, down_made, added = (st.sem(n) for n in ("h_turned", "h_kept", "down_made", "added"))
        xg, staged = st.sb("xg", [128, GT]), st.sem("staged")
        V = nc.vector
        hv = hid[:].rearrange("p (b f) -> p b f", f=F0)
        wv = wraw[:].rearrange("p (c k) -> p c k", k=128)
        with nc.Block() as block:
            @block.sync
            def _(sp):
                sp.dma_start(wdraw[:], a["L0_ffn_w_down"]).then_inc(loaded, 16)
                sp.wait_ge(cleared, 1)
                for w, name in enumerate(("L0_ffn_w_gate", "L0_ffn_w_up")):
                    for k, (k0, kn) in enumerate(KC):
                        sp.dma_start(wv[0:kn, 3 * w + k, :], a[name][k0:k0 + kn, :]).then_inc(loaded, 16)

            @block.vector
            def _(dve):
                V.memset(wraw[:], 0.0).then_inc(cleared, 1)
                quantise(nc, dve, order, m.xn[:].rearrange("p b d -> p (b d)"), mag[:], lev[:], sc[:], NB * D // 16)
                ins = V.memset(ht[:], 0.0)
                ins.then_inc(x_quant, 1)
                dve.wait_ge(loaded, 7 * 16)
                n = 7 * 128
                quantise(nc, dve, order, wraw[:], mag[:, 0:n], lev[:, 0:n], sc[:, :, 0:n // 16], n // 16)
                quantise(nc, dve, order, wdraw[:], mag[:, 0:F0], lev[:, 0:F0], sc[:, :, 0:F0 // 16], F0 // 16)
                V.tensor_copy(lev[:, 0:1], wdraw[:, 0:1]).then_inc(w_quant, 1)
                for g in range(1, NG, 2):
                    dve.wait_ge(x_turned, g + 1)
                    V.tensor_copy(m.xt[:, g * GT:(g + 1) * GT], m.ps[:, g, :]).then_inc(x_kept, 1)
                dve.wait_ge(w_turned, 3)
                V.tensor_copy(wgt[:], m.ps[:, 0, 0:384])
                V.tensor_copy(wut[:], m.ps[:, 1, 0:384])
                V.tensor_copy(wdt[:].rearrange("p a b -> p (a b)"), m.ps[:, 2, 0:384]).then_inc(w_kept, 1)
                done = order.n
                per = QUANTISE_STEPS
                with V.Fori(0, NG) as g:
                    order.turn(done, g, per)
                    dve.wait_ge(silu_made, g + 1)
                    dve.wait_ge(up_made, g + 1)
                    V.tensor_tensor(hv, gate[:], m.ps[:, 4:8, 0:F0], ALU.mult).then_inc(h_made, 1)
                    dve.wait_ge(h_made, g + 1)
                    n = GB * F0
                    quantise(nc, dve, order, hid[:], mag[:, 0:n], lev[:, 0:n], sc[:, :, 0:n // 16], n // 16)
                    V.tensor_copy(lev[:, 0:1], hid[:, 0:1]).then_inc(h_quant, 1)
                    dve.wait_ge(down_made, g + 1)
                    xs = m.x[:, bass.ts(g, GB), :]
                    V.tensor_tensor(xs, xs, m.ps[:, 3, :].rearrange("p (b c) -> p b c", c=D),
                                    ALU.add).then_inc(added, 1)
                order.turned(done, NG, per)
                dve.wait_ge(added, NG)

            @block.gpsimd
            def _(pool):
                stage_groups(nc, xg, m.xt, staged, up_made, x_kept, NG)(pool)

            @block.tensor
            def _(pe):
                pe.wait_ge(x_quant, 1)
                for g in range(NG):
                    for j in range(GB):
                        ins = nc.tensor.transpose(m.ps[:, g, j * T:(j + 1) * T], m.xn[:, GB * g + j, :], m.ident[:])
                    ins.then_inc(x_turned, 1)
                pe.wait_ge(w_quant, 1)
                pe.wait_ge(x_kept, NG)
                for w in range(2):
                    for k in range(3):
                        ins = nc.tensor.transpose(m.ps[:, w, k * 128:(k + 1) * 128], wv[:, 3 * w + k, :], m.ident[:])
                    ins.then_inc(w_turned, 1)
                for k, (k0, kn) in enumerate(KC):
                    ins = nc.tensor.matmul(m.ps[0:kn, 2, k * 128:(k + 1) * 128], wdraw[:, k0:k0 + kn], m.ident[:],
                                           start=True, stop=True)
                ins.then_inc(w_turned, 1)
                pe.wait_ge(w_kept, 1)
                with nc.tensor.Fori(0, NG) as g:
                    pe.wait_ge(h_kept, g)
                    pe.wait_ge(added, g)
                    pe.wait_ge(staged, g + 1)
                    for j in range(GB):
                        xb = xg[:, j * T:(j + 1) * T]
                        nc.tensor.matmul(m.ps[:, j, 0:F0], xb, wgt[:, 0:F0], start=True, stop=True)
                        ins = nc.tensor.matmul(m.ps[:, 4 + j, 0:F0], xb, wut[:, 0:F0], start=True, stop=True)
                    ins.then_inc(up_made, 1)
                    pe.wait_ge(h_quant, g + 1)
                    for k, (k0, kn) in enumerate(KC):
                        for j in range(GB):
                            ins = nc.tensor.transpose(m.ps[0:kn, k, j * T:(j + 1) * T], hv[:, j, k0:k0 + kn],
                                                      m.ident[:])
                    ins.then_inc(h_turned, 1)
                    pe.wait_ge(h_kept, g + 1)
                    for j in range(GB):
                        for k, (k0, kn) in enumerate(KC):
                            ins = nc.tensor.matmul(m.ps[:, 3, j * T:(j + 1) * T], ht[0:kn, k, j * T:(j + 1) * T],
                                                   wdt[0:kn, k, :], start=(k == 0), stop=(k == 2))
                    ins.then_inc(down_made, 1)

            @block.scalar
            def _(act):
                for g in range(0, NG, 2):
                    act.wait_ge(x_turned, g + 1)
                    nc.scalar.copy(m.xt[:, g * GT:(g + 1) * GT], m.ps[:, g, :]).then_inc(x_kept, 1)
                with nc.scalar.Fori(0, NG) as g:
                    act.wait_ge(up_made, g + 1)
                    nc.scalar.activation(gate[:], m.ps[:, 0:4, 0:F0], ACT.Silu).then_inc(silu_made, 1)
                    act.wait_ge(h_turned, g + 1)
                    nc.scalar.copy(ht[:, 0:2, :], m.ps[:, 0:2, :])
                    nc.scalar.copy(ht[0:96, 2, :], m.ps[0:96, 2, :]).then_inc(h_kept, 1)


H1, HD1 = 16, 64
KV1 = H1 * HD1
NC1 = KV1 // 128
QUADS, LEVELS = 4, 7
TINY = 1e-18


def l1_decay_stage(nc, m, a, g_all, beta):
    with Stage(nc, "l1g") as st:
        wba = st.sb("wba", [128, 2 * H1])
        bias, rate = st.sb("bias", [128, H1]), st.sb("rate", [128, H1])
        full = [128, NB, H1]
        y, neg, ex, u, ln = (st.sb(n, full) for n in ("y", "neg", "ex", "u", "ln"))
        loaded, made, shifted, exped = (st.sem(n) for n in ("loaded", "made", "shifted", "exped"))
        one_more, logged, order = st.sem("one_more"), st.sem("logged"), Chain(st.sem("dve_order"))
        V = nc.vector
        bp = m.ps[:, 0:2, :].rearrange("p a (b h) -> p (a b) h", h=2 * H1)
        with nc.Block() as block:
            @block.sync
            def _(sp):
                sp.dma_start(wba[:], a["L1_attn_W_ba"]).then_inc(loaded, 16)
                sp.dma_start(bias[:], over(a["L1_attn_dt_bias"].unsqueeze(0), 128, H1)).then_inc(loaded, 16)
                sp.dma_start(rate[:], over(a["L1_attn_A_log"].unsqueeze(0), 128, H1)).then_inc(loaded, 16)

            @block.tensor
            def _(pe):
                pe.wait_ge(loaded, 48)
                for b in range(NB):
                    ins = nc.tensor.matmul(bp[:, b, :], m.xt[:, b * T:(b + 1) * T], wba[:], start=True, stop=True)
                ins.then_inc(made, 1)

            @block.vector
            def _(dve):
                dve.wait_ge(loaded, 48)
                order(dve, V.tensor_scalar(rate[:], rate[:], -2.3, None, ALU.max))
                dve.wait_ge(made, 1)
                order(dve, V.tensor_tensor(y[:], bp[:, :, H1:2 * H1], over(bias[:].unsqueeze(1), *full), ALU.add))
                order(dve, V.scalar_tensor_tensor(out=neg[:], in0=y[:], scalar=-1.0, in1=y[:], op0=ALU.mult,
                                                  op1=ALU.min))
                V.tensor_scalar(y[:], y[:], 0.0, None, ALU.max).then_inc(shifted, 1)
                dve.wait_ge(exped, 1)
                V.tensor_scalar(u[:], ex[:], 1.0, None, ALU.add).then_inc(one_more, 1)
                dve.wait_ge(logged, 1)
                order(dve, V.tensor_scalar(neg[:], u[:], 1.0, 1e-30, ALU.subtract, ALU.max))
                order(dve, V.reciprocal(neg[:], neg[:]))
                order(dve, V.tensor_tensor(ln[:], ln[:], ex[:], ALU.mult))
                order(dve, V.tensor_tensor(ln[:], ln[:], neg[:], ALU.mult))
                order(dve, V.scalar_tensor_tensor(out=u[:], in0=u[:], scalar=1.0, in1=ex[:], op0=ALU.is_equal,
                                                  op1=ALU.mult))
                order(dve, V.tensor_tensor(ln[:], ln[:], u[:], ALU.add))
                order(dve, V.tensor_tensor(y[:], y[:], ln[:], ALU.add))
                order(dve, V.scalar_tensor_tensor(out=g_all[:], in0=y[:], scalar=-1.0,
                                                  in1=over(rate[:].unsqueeze(1), *full), op0=ALU.mult,
                                                  op1=ALU.mult))

            @block.scalar
            def _(act):
                act.wait_ge(shifted, 1)
                nc.scalar.activation(rate[:], rate[:], ACT.Exp)
                nc.scalar.activation(ex[:], neg[:], ACT.Exp).then_inc(exped, 1)
                act.wait_ge(one_more, 1)
                nc.scalar.activation(ln[:], u[:], ACT.Ln).then_inc(logged, 1)
                nc.scalar.activation(beta[:], bp[:, :, 0:H1], ACT.Sigmoid).then_inc(logged, 1)
                act.wait_ge(logged, 2)


def l1_attn_stage(nc, m, a):
    with Stage(nc, "l1a") as st:
        g_all, beta = st.sb("g_all", [128, NB, H1]), st.sb("beta", [128, NB, H1])
        l1_decay_stage(nc, m, a, g_all, beta)
        w_in, w_o = st.sb("w_in", [128, 4 * KV1]), st.sb("w_o", [128, NC1, D])
        taps, norm_w = st.sb("taps", [128, 3 * NC1, 4]), st.sb("norm_w", [128, HD1])
        strict, levels, pair = st.sb("strict", [128, 128]), st.sb("levels", [128, LEVELS, 128]), st.sb("pair", [128, 2])
        cin = st.sb("cin", [128, 3 * NC1, T + 3])
        qkv = st.sb("qkv", [128, 3 * NC1, T])
        ta, tb, tc = (st.sb(n, [128, NC1, T]) for n in ("ta", "tb", "tc"))
        free = m.xn[:].rearrange("p b d -> p (b d)")
        gm = free[:, 0:H1 * T].rearrange("p (h s) -> p h s", h=H1)
        sq = free[:, H1 * T:2 * H1 * T].rearrange("p (c t) -> p c t", t=T)
        zs, v2, o = st.sb("zs", [128, KV1]), st.sb("v2", [128, KV1]), st.sb("o", [128, KV1])
        ot = st.sb("ot", [128, NC1, T])
        xg = st.sb("xg", [128, T])
        quad = [128, 4, T]
        e_, a_, p_, inv, inv_t, y_ = ([st.sb(f"{n}{s}", quad) for s in range(2)]
                                      for n in ("e", "a", "p", "inv", "inv_t", "y"))
        q_ = [[st.sb(f"q{s}_{r}", quad) for r in range(2)] for s in range(2)]
        w_ = [st.sb(f"w{s}", [128, 4, HD1]) for s in range(2)]
        ss, root, rk2, cs, rq = (st.sb(n, [128, 2 * H1]) for n in ("ss", "root", "rk2", "cs", "rq"))
        om = st.sb("om", [128, 2, H1])
        S = {n: st.sem(n) for n in (
            "loaded", "padded", "staged", "projected", "conv_in", "z_made", "z_silu", "z_scaled", "taps_pool",
            "conv_sum", "silu", "squared", "sums", "v_turned", "eps_added", "rooted", "scales", "v_scaled",
            "g_masked", "d_made", "d_exp", "e_made", "kk_made", "ap_made", "q_made", "inv_first", "inv_turned",
            "inv_ready", "y_made", "y_kept", "step_made", "w_made", "w_kept", "o_made", "o_kept", "o_squared",
            "o_mean", "o_root", "o_gated", "o_turned", "o_copied", "out_made", "added")}
        dchain, pchain = Chain(st.sem("dve_order")), Chain(st.sem("pool_order"))
        V, A_, P_, E_ = nc.vector, nc.scalar, nc.gpsimd, nc.tensor
        ps = m.ps
        Dp, KKp, KQp, Ip = (lambda s: ps[:, 4 * s, :]), (lambda s: ps[:, 4 * s + 1, :]), \
            (lambda s: ps[:, 4 * s + 2, :]), (lambda s: ps[:, 4 * s + 3, :])
        q4 = lambda t: t.rearrange("p (h t) -> p h t", t=T)
        heads_by_half = lambda s: ps[:, 4 * s + 1:4 * s + 3, :].rearrange("p half (k i t) -> p k i half t", k=2, t=T)
        vt = ps[:, 0:2, :].rearrange("p a b -> p (a b)")
        with nc.Block() as block:
            @block.sync
            def _(sp):
                sp.dma_start(w_in[:], a["L1_attn_W_in"]).then_inc(S["loaded"], 16)
                sp.dma_start(w_o[:], a["L1_attn_W_o"].rearrange("(c p) n -> p c n", p=128)).then_inc(S["loaded"], 16)
                sp.dma_start(taps[:], a["L1_attn_conv_w"].rearrange("(c p) o k -> p c (o k)", p=128)).then_inc(S["loaded"], 16)
                sp.dma_start(norm_w[:], over(a["L1_attn_norm_w"].unsqueeze(0), 128, HD1)).then_inc(S["loaded"], 16)
                sp.dma_start(strict[:], a["c_strict"]).then_inc(S["loaded"], 16)
                sp.dma_start(levels[:], a["c_levels"]).then_inc(S["loaded"], 16)
                sp.dma_start(pair[:], a["c_pair"]).then_inc(S["loaded"], 16)
            LOADED = 7 * 16

            @block.gpsimd
            def _(pool):
                P_.memset(cin[:], 0.0).then_inc(S["padded"], 1)
                pool.wait_ge(S["loaded"], LOADED)
                with P_.Fori(0, NB) as b:
                    pool.wait_ge(S["z_made"], b)
                    pool.wait_ge(S["loaded"], LOADED)
                    P_.tensor_copy(xg[:], m.xt[:, bass.ts(b, T)]).then_inc(S["staged"], 1)
                    pool.wait_ge(S["d_made"], b * QUADS)
                    P_.tensor_tensor(gm, over(strict[:].unsqueeze(1), 128, H1, T),
                                     over(g_all[:, bass.ds(b, 1), :].rearrange("p o h -> p (o h)").unsqueeze(2), 128, H1, T),
                                     ALU.mult).then_inc(S["g_masked"], 1)
                    pchain.turn(0, b, 6)
                    for i in range(3):
                        pool.wait_ge(S["conv_in"], b * 6 + 2 * i + 2)
                        pool.wait_ge(S["conv_sum"], b * 3 + i)
                        r = slice(NC1 * i, NC1 * i + NC1)
                        w = lambda k: over(taps[:, r, k:k + 1], 128, NC1, T)
                        pchain(pool, P_.tensor_tensor(ta[:], cin[:, r, 0:T], w(0), ALU.mult))
                        pchain(pool, P_.tensor_tensor(tb[:], cin[:, r, 1:1 + T], w(1), ALU.mult))
                        P_.tensor_tensor(ta[:], ta[:], tb[:], ALU.add).then_inc(S["taps_pool"], 1)
                        pool.wait_ge(S["taps_pool"], b * 3 + i + 1)
                    pool.wait_ge(S["z_silu"], b + 1)
                    P_.tensor_tensor(zs[:].rearrange("p (h d) -> p h d", d=HD1), zs[:].rearrange("p (h d) -> p h d", d=HD1),
                                     over(norm_w[:].unsqueeze(1), 128, H1, HD1), ALU.mult).then_inc(S["z_scaled"], 1)
                    for hf in range(2):
                        for l in range(LEVELS):
                            for s in range(2):
                                u = hf * 2 + s
                                pool.wait_ge(S["ap_made"], b * QUADS + u + 1)
                                if l < 2:
                                    pool.wait_ge(S["y_made"], b * 24 + hf * 12)
                                elif l == 2:
                                    pool.wait_ge(S["inv_first"], b * QUADS + u + 1)
                                else:
                                    pool.wait_ge(S["y_made"], b * 24 + hf * 12 + (l - 3) * 2 + s + 1)
                                P_.tensor_tensor(q_[s][l % 2][:], a_[s][:], over(levels[:, l:l + 1, :], *quad),
                                                 ALU.mult).then_inc(S["q_made"], 1)

            @block.tensor
            def _(pe):
                pe.wait_ge(S["loaded"], LOADED)
                with E_.Fori(0, NB) as b:
                    pe.wait_ge(S["added"], b)
                    for c in range(3 * NC1):
                        ins = E_.matmul(ps[:, c // 4, (c % 4) * T:(c % 4 + 1) * T], w_in[:, c * 128:(c + 1) * 128],
                                        m.xt[:, bass.ts(b, T)], start=True, stop=True)
                        if c % 4 == 3:
                            ins.then_inc(S["projected"], 1)
                    pe.wait_ge(S["staged"], b + 1)
                    for c in range(2):
                        ins = E_.matmul(ps[:, 6 + c, :], xg[:], w_in[:, 3 * KV1 + 512 * c:3 * KV1 + 512 * (c + 1)],
                                        start=True, stop=True)
                    ins.then_inc(S["z_made"], 1)
                    pe.wait_ge(S["z_silu"], b + 1)
                    pe.wait_ge(S["squared"], b + 1)
                    for c in range(2 * NC1):
                        ins = E_.matmul(ps[:, 6, 2 * c:2 * c + 2], sq[:, c, :], pair[:], start=True, stop=True)
                    ins.then_inc(S["sums"], 1)
                    pe.wait_ge(S["silu"], 3 * b + 3)
                    for c in range(NC1):
                        ins = E_.transpose(vt[:, c * 128:(c + 1) * 128], qkv[:, 2 * NC1 + c, :], m.ident[:])
                    ins.then_inc(S["v_turned"], 1)
                    pe.wait_ge(S["g_masked"], b + 1)
                    pe.wait_ge(S["v_scaled"], b + 1)
                    for hf in range(2):
                        for s in range(2):
                            u = hf * 2 + s
                            if hf:
                                pe.wait_ge(S["o_kept"], b * QUADS + s + 1)
                            for j in range(4):
                                ins = E_.matmul(q4(Dp(s))[:, j, :], gm[:, 4 * u + j, :], m.causal[:], start=True, stop=True)
                            ins.then_inc(S["d_made"], 1)
                            for j in range(4):
                                h = 4 * u + j
                                r, c = slice(64 * (h % 2), 64 * (h % 2) + 64), h // 2
                                out = heads_by_half(s)
                                E_.matmul(out[:, 0, j // 2, j % 2, :], qkv[r, NC1 + c, :], qkv[r, NC1 + c, :], start=True, stop=True)
                                ins = E_.matmul(out[:, 1, j // 2, j % 2, :], qkv[r, NC1 + c, :], qkv[r, c, :], start=True, stop=True)
                            ins.then_inc(S["kk_made"], 1)
                        for s in range(2):
                            pe.wait_ge(S["inv_first"], b * QUADS + hf * 2 + s + 1)
                            for j in range(4):
                                ins = E_.transpose(q4(Ip(s))[:, j, :], inv_t[s][:, j, :], m.ident[:])
                            ins.then_inc(S["inv_turned"], 1)
                        for l in range(1, LEVELS):
                            for s in range(2):
                                n = b * 28 + hf * 14 + (l - 1) * 2 + s + 1
                                pe.wait_ge(S["inv_ready"], n)
                                pe.wait_ge(S["q_made"], b * 28 + hf * 14 + l * 2 + s + 1)
                                for j in range(4):
                                    ins = E_.matmul(q4(Dp(s))[:, j, :], q_[s][l % 2][:, j, :], inv[s][:, j, :],
                                                    start=True, stop=True)
                                ins.then_inc(S["y_made"], 1)
                            for s in range(2):
                                pe.wait_ge(S["y_kept"], b * 24 + hf * 12 + (l - 1) * 2 + s + 1)
                                for j in range(4):
                                    ins = E_.matmul(q4(KKp(s))[:, j, :], y_[s][:, j, :], inv_t[s][:, j, :],
                                                    start=True, stop=True)
                                if l < LEVELS - 1:
                                    for j in range(4):
                                        ins = E_.matmul(q4(KQp(s))[:, j, :], inv_t[s][:, j, :], y_[s][:, j, :],
                                                        start=True, stop=True)
                                ins.then_inc(S["step_made"], 1)
                        for s in range(2):
                            pe.wait_ge(S["inv_ready"], b * 28 + hf * 14 + 12 + s + 1)
                            for j in range(4):
                                h = 4 * (hf * 2 + s) + j
                                ins = E_.matmul(Ip(s)[:, j * HD1:(j + 1) * HD1], inv_t[s][:, j, :],
                                                v2[:, h * HD1:(h + 1) * HD1], start=True, stop=True)
                            ins.then_inc(S["w_made"], 1)
                        for s in range(2):
                            pe.wait_ge(S["w_kept"], b * QUADS + hf * 2 + s + 1)
                            for j in range(4):
                                ins = E_.matmul(Ip(s)[:, 256 + j * HD1:256 + (j + 1) * HD1], p_[s][:, j, :],
                                                w_[s][:, j, :], start=True, stop=True)
                            ins.then_inc(S["o_made"], 1)
                    pe.wait_ge(S["o_gated"], b + 1)
                    for c in range(NC1):
                        ins = E_.transpose(vt[:, c * 128:(c + 1) * 128], o[:, c * 128:(c + 1) * 128], m.ident[:])
                    ins.then_inc(S["o_turned"], 1)
                    pe.wait_ge(S["o_copied"], b + 1)
                    for c in range(NC1):
                        ins = E_.matmul(ps[:, 2, 0:D], ot[:, c, :], w_o[:, c, :], start=(c == 0), stop=(c == NC1 - 1))
                    ins.then_inc(S["out_made"], 1)

            @block.scalar
            def _(act):
                act.wait_ge(S["padded"], 1)
                with A_.Fori(0, NB) as b:
                    for i in range(6):
                        act.wait_ge(S["projected"], b * 6 + i + 1)
                        if i == 0:
                            act.wait_ge(S["taps_pool"], 3 * b)
                            act.wait_ge(S["conv_sum"], 3 * b)
                        A_.copy(cin[:, 4 * i:4 * i + 4, 3:3 + T], q4(ps[:, i, :])).then_inc(S["conv_in"], 1)
                    act.wait_ge(S["z_made"], b + 1)
                    act.wait_ge(S["o_gated"], b)
                    A_.activation(zs[:], ps[:, 6:8, :], ACT.Silu).then_inc(S["z_silu"], 1)
                    for i in range(3):
                        act.wait_ge(S["conv_sum"], b * 3 + i + 1)
                        r = slice(NC1 * i, NC1 * i + NC1)
                        A_.activation(qkv[:, r, :], qkv[:, r, :], ACT.Silu).then_inc(S["silu"], 1)
                    act.wait_ge(S["silu"], 3 * b + 2)
                    A_.activation(sq, qkv[:, 0:2 * NC1, :], ACT.Square).then_inc(S["squared"], 1)
                    act.wait_ge(S["eps_added"], b + 1)
                    A_.activation(root[:], ss[:], ACT.Sqrt).then_inc(S["rooted"], 1)
                    for hf in range(2):
                        for s in range(2):
                            act.wait_ge(S["d_made"], b * QUADS + hf * 2 + s + 1)
                            act.wait_ge(S["ap_made"], b * QUADS + hf * 2 + (s if hf else 0))
                            A_.activation(e_[s][:], q4(Dp(s)), ACT.Exp).then_inc(S["d_exp"], 1)
                        for s in range(2):
                            act.wait_ge(S["inv_turned"], b * QUADS + hf * 2 + s + 1)
                            A_.copy(inv[s][:], q4(Ip(s))).then_inc(S["inv_ready"], 1)
                        for l in range(1, LEVELS):
                            for s in range(2):
                                act.wait_ge(S["y_made"], b * 24 + hf * 12 + (l - 1) * 2 + s + 1)
                                A_.activation(y_[s][:], q4(Dp(s)), ACT.Copy, bias=TINY).then_inc(S["y_kept"], 1)
                        for s in range(2):
                            act.wait_ge(S["w_made"], b * QUADS + hf * 2 + s + 1)
                            A_.copy(w_[s][:], Ip(s)[:, 0:256].rearrange("p (h d) -> p h d", d=HD1)).then_inc(S["w_kept"], 1)
                    act.wait_ge(S["o_kept"], QUADS * (b + 1))
                    A_.activation(ta[:].rearrange("p a b -> p (a b)"), o[:], ACT.Square).then_inc(S["o_squared"], 1)
                    act.wait_ge(S["o_mean"], b + 1)
                    A_.activation(om[:, 1, :], om[:, 0, :], ACT.Sqrt).then_inc(S["o_root"], 1)
                    act.wait_ge(S["o_turned"], b + 1)
                    A_.copy(ot[:], vt.rearrange("p (c t) -> p c t", t=T)).then_inc(S["o_copied"], 1)

            @block.vector
            def _(dve):
                dve.wait_ge(S["loaded"], LOADED)
                per = 6 + 3 + 8 + 3
                with V.Fori(0, NB) as b:
                    dchain.turn(0, b, per)
                    for i in range(3):
                        dve.wait_ge(S["conv_in"], b * 6 + 2 * i + 2)
                        r = slice(NC1 * i, NC1 * i + NC1)
                        w = lambda k: over(taps[:, r, k:k + 1], 128, NC1, T)
                        V.tensor_tensor(tc[:], cin[:, r, 2:2 + T], w(2), ALU.mult)
                        dchain(dve, V.tensor_tensor(qkv[:, r, :], cin[:, r, 3:3 + T], w(3), ALU.mult))
                        dchain(dve, V.tensor_tensor(qkv[:, r, :], qkv[:, r, :], tc[:], ALU.add))
                        dve.wait_ge(S["taps_pool"], b * 3 + i + 1)
                        V.tensor_tensor(qkv[:, r, :], qkv[:, r, :], ta[:], ALU.add).then_inc(S["conv_sum"], 1)
                        dve.wait_ge(S["conv_sum"], b * 3 + i + 1)
                    dve.wait_ge(S["sums"], b + 1)
                    V.tensor_scalar(ss[:], ps[:, 6, 0:2 * H1], 1e-6, None, ALU.add).then_inc(S["eps_added"], 1)
                    dve.wait_ge(S["eps_added"], b + 1)
                    dchain(dve, V.reciprocal(rk2[:], ss[:]))
                    dchain(dve, V.tensor_tensor(cs[:, 0:H1], rk2[:, H1:2 * H1],
                                                beta[:, bass.ds(b, 1), :].rearrange("p o h -> p (o h)"), ALU.mult))
                    dve.wait_ge(S["rooted"], b + 1)
                    dchain(dve, V.reciprocal(rq[:], root[:]))
                    V.tensor_scalar(rq[:, 0:H1], rq[:, 0:H1], HD1 ** -0.5, None, ALU.mult).then_inc(S["scales"], 1)
                    dve.wait_ge(S["v_turned"], b + 1)
                    V.tensor_tensor(v2[:].rearrange("p (h d) -> p h d", d=HD1), vt.rearrange("p (h d) -> p h d", d=HD1),
                                    over(root[:, H1:2 * H1].unsqueeze(2), 128, H1, HD1), ALU.mult).then_inc(S["v_scaled"], 1)
                    dve.wait_ge(S["scales"], b + 1)
                    for hf in range(2):
                        for s in range(2):
                            u = hf * 2 + s
                            dve.wait_ge(S["d_exp"], b * QUADS + u + 1)
                            dchain(dve, V.scalar_tensor_tensor(out=e_[s][:], in0=e_[s][:], scalar=TINY,
                                                               in1=over(m.causal[:].unsqueeze(1), *quad),
                                                               op0=ALU.max, op1=ALU.mult))
                            dchain(dve, V.tensor_tensor(e_[s][:], e_[s][:],
                                                        over(cs[:, 4 * u:4 * u + 4].unsqueeze(2), *quad), ALU.mult))
                            dve.wait_ge(S["kk_made"], b * QUADS + u + 1)
                            dve.wait_ge(S["q_made"], b * 28 + hf * 14)
                            h4 = lambda t: t[:].rearrange("p (i half) t -> p i half t", half=2)
                            V.tensor_tensor(h4(a_[s]), h4(e_[s]), heads_by_half(s)[:, 0], ALU.mult)
                            V.tensor_tensor(h4(p_[s]), h4(e_[s]), heads_by_half(s)[:, 1], ALU.mult).then_inc(S["ap_made"], 1)
                        for s in range(2):
                            dve.wait_ge(S["q_made"], b * 28 + hf * 14 + s + 1)
                            V.tensor_tensor(inv_t[s][:], over(m.ident[:].unsqueeze(1), *quad), q_[s][0][:],
                                            ALU.subtract).then_inc(S["inv_first"], 1)
                        for l in range(1, LEVELS):
                            for s in range(2):
                                dve.wait_ge(S["step_made"], b * 24 + hf * 12 + (l - 1) * 2 + s + 1)
                                if l < LEVELS - 1:
                                    V.tensor_tensor(inv[s][:], inv[s][:], q4(KQp(s)), ALU.subtract)
                                V.tensor_tensor(inv_t[s][:], inv_t[s][:], q4(KKp(s)), ALU.subtract).then_inc(S["inv_ready"], 1)
                        for s in range(2):
                            u = hf * 2 + s
                            dve.wait_ge(S["o_made"], b * QUADS + u + 1)
                            V.tensor_tensor(o[:, 256 * u:256 * u + 256].rearrange("p (h d) -> p h d", d=HD1),
                                            Ip(s)[:, 256:512].rearrange("p (h d) -> p h d", d=HD1),
                                            over(rq[:, 4 * u:4 * u + 4].unsqueeze(2), 128, 4, HD1),
                                            ALU.mult).then_inc(S["o_kept"], 1)
                    dve.wait_ge(S["o_squared"], b + 1)
                    dchain(dve, V.tensor_reduce(om[:, 0, :], ta[:].rearrange("p a b -> p (a b)").rearrange(
                        "p (h d) -> p h d", d=HD1), AX.X, ALU.add))
                    V.tensor_scalar(om[:, 0, :], om[:, 0, :], 1.0 / HD1, 1e-6, ALU.mult, ALU.add).then_inc(S["o_mean"], 1)
                    dve.wait_ge(S["o_root"], b + 1)
                    dchain(dve, V.reciprocal(om[:, 0, :], om[:, 1, :]))
                    dchain(dve, V.tensor_tensor(o[:].rearrange("p (h d) -> p h d", d=HD1),
                                                o[:].rearrange("p (h d) -> p h d", d=HD1),
                                                over(om[:, 0, :].unsqueeze(2), 128, H1, HD1), ALU.mult))
                    dve.wait_ge(S["z_scaled"], b + 1)
                    V.tensor_tensor(o[:], o[:], zs[:], ALU.mult).then_inc(S["o_gated"], 1)
                    dve.wait_ge(S["out_made"], b + 1)
                    xs = m.x[:, bass.ds(b, 1), :].rearrange("p o d -> p (o d)")
                    V.tensor_tensor(xs, xs, ps[:, 2, 0:D], ALU.add).then_inc(S["added"], 1)
                    assert dchain.n == per, dchain.n
                dve.wait_ge(S["added"], NB)


def head_attn_stage(nc, m, a, name, mode, wq, wk, wv, wo, keys, target, bq=None, bk=None, bv=None, bo=None):
    softmax = mode != "linear"
    HB = H // 2
    with Stage(nc, name) as st:
        w = {n: st.sb(f"w{n}", [128, D]) for n in "qkvo"}
        biases = {n: v for n, v in zip("qkvo", (bq, bk, bv, bo)) if v is not None}
        bias = {n: st.sb(f"b{n}", [1, D]) for n in biases}
        hmask = st.sb("hmask", [128, H])
        xg = st.sb("xg", [128, GT])
        qt, kt = st.sb("qt", [128, GT]), st.sb("kt", [128, GT])
        low = st.sb("low", [128, 2, GT])
        spread = [st.sb(f"spread{i}", [128, H, T]) for i in range(2)]
        v1 = st.sb("v1", [128, GB, H, HD + 1])
        prob = [st.sb(f"prob{i}", [128, H, T]) for i in range(2)]
        turned = st.sb("turned", [128, H, T])
        top = st.sb("top", [128, 2, H])
        rec, o, ot = st.sb("rec", [128, H]), st.sb("o", [128, 2, D]), st.sb("ot", [128, GT])
        neg = st.sb("neg", [128, NB if mode == "masked" else 1, T])
        mask_in = st.sb("mask_in", [128, NB, T], I32) if mode == "masked" else None
        S = {n: st.sem(n) for n in (
            "loaded", "masked", "ones_set", "staged", "q_made", "k_made", "v_made", "q_low", "k_low", "q_exp", "k_exp",
            "q_kept", "k_kept", "v_kept", "spread", "scores", "max_taken", "shifted", "weights", "turned", "turned_kept",
            "read", "normed", "o_turned", "o_kept", "out_made", "added")}
        dchain = Chain(st.sem("dve_order"))
        V, A_, P_, E_ = nc.vector, nc.scalar, nc.gpsimd, nc.tensor
        ps = m.ps
        n_load = 16 * (5 + len(bias) + 1)
        hv = lambda t: t.rearrange("p (h t) -> p h t", t=T)
        score = lambda hf: ps[:, 2 * hf:2 * hf + 2, :].rearrange("p a (h t) -> p (a h) t", t=T)
        tp = ps[:, 4:6, :].rearrange("p a (h t) -> p (a h) t", t=T)
        read = ps[:, 6, 0:H * (HD + 1)].rearrange("p (h d) -> p h d", d=HD + 1)
        otp, big = ps[:, 7, 0:T], ps[:, 7, :]
        with nc.Block() as block:
            @block.sync
            def _(sp):
                for n, src in zip("qkvo", (wq, wk, wv, wo)):
                    sp.dma_start(w[n][:], src).then_inc(S["loaded"], 16)
                for n in bias:
                    sp.dma_start(bias[n][:], biases[n].unsqueeze(0)).then_inc(S["loaded"], 16)
                sp.dma_start(hmask[:], a["c_hmask"]).then_inc(S["loaded"], 16)
                if mode == "masked":
                    sp.dma_start(mask_in[:], a["mask_Bx1xSxS2_ik1"].rearrange("b o q k -> q (b o) k")).then_inc(S["loaded"], 16)
                else:
                    sp.dma_start(neg[:], a["c_future"].unsqueeze(1)).then_inc(S["loaded"], 16)

            @block.gpsimd
            def _(pool):
                pool.wait_ge(S["loaded"], n_load)
                src = spread
                with P_.Fori(0, NG) as g:
                    pool.wait_ge(S["v_made"], g)
                    pool.wait_ge(S["loaded"], n_load)
                    P_.tensor_copy(xg[:], keys[:, bass.ts(g, GT)]).then_inc(S["staged"], 1)
                    pool.wait_ge(S["k_kept"] if softmax else S["q_kept"], g + 1)
                    for j in range(GB):
                        n = g * GB + j
                        pool.wait_ge(S["scores"], 2 * (g * GB + max(j - 1, 0)))
                        side = kt if softmax else qt
                        P_.tensor_tensor(spread[j % 2][:], over(side[:, j * T:(j + 1) * T].unsqueeze(1), 128, H, T),
                                         over(hmask[:].unsqueeze(2), 128, H, T), ALU.mult).then_inc(S["spread"], 1)

            @block.tensor
            def _(pe):
                pe.wait_ge(S["loaded"], n_load)
                if softmax:
                    pe.wait_ge(S["masked"], 1)

                def project(out, n, moving, sem):
                    ins = E_.matmul(out, w[n][:], moving, start=True, stop=n not in bias)
                    if n in bias:
                        ins = E_.matmul(out, bias[n][:], m.ones[0:1, :], start=False, stop=True)
                    ins.then_inc(sem, 1)

                def scores(g, j):
                    pe.wait_ge(S["spread"], g * GB + j + 1)
                    if j == 0:
                        pe.wait_ge(S["q_kept"], g + 1)
                        pe.wait_ge(S["k_kept"], g + 1)
                    side = qt if softmax else kt
                    for hf in range(2):
                        pe.wait_ge(S["shifted"], 2 * (g * GB + j) if hf == 0 and j == 0 else 2 * (g * GB + j) + hf - 1)
                        for i in range(2):
                            h = slice(HB * hf + 4 * i, HB * hf + 4 * i + 4)
                            ins = E_.matmul(ps[:, 2 * hf + i, :], side[:, j * T:(j + 1) * T], spread[j % 2][:, h, :],
                                            start=True, stop=not softmax)
                            if softmax:
                                mask = neg[:, bass.ds(g * GB + j, 1), :] if mode == "masked" else neg[:]
                                ins = E_.matmul(ps[:, 2 * hf + i, :], m.ident[:], over(mask, 128, 4, T), start=False,
                                                stop=True)
                        ins.then_inc(S["scores"], 1)

                with E_.Fori(0, NG) as g:
                    pe.wait_ge(S["added"], g)
                    pe.wait_ge(S["o_kept"], GB * g)
                    project(big, "q", m.xt[:, bass.ts(g, GT)], S["q_made"])
                    pe.wait_ge(S["q_kept"], g + 1)
                    project(big, "k", keys[:, bass.ts(g, GT)], S["k_made"])
                    pe.wait_ge(S["staged"], g + 1)
                    pe.wait_ge(S["k_kept"], g + 1)
                    for j in range(GB):
                        c = slice(j * T, (j + 1) * T)
                        ins = E_.matmul(big[:, c], xg[:, c], w["v"][:], start=True, stop="v" not in bias)
                        if "v" in bias:
                            ins = E_.matmul(big[:, c], m.ones[0:1, 0:T], bias["v"][:], start=False, stop=True)
                    ins.then_inc(S["v_made"], 1)
                    scores(g, 0)
                    for j in range(GB):
                        n = g * GB + j
                        if j < GB - 1:
                            scores(g, j + 1)
                        if softmax:
                            for hf in range(2):
                                pe.wait_ge(S["weights"], 2 * n + hf + 1)
                                pe.wait_ge(S["turned_kept"], 2 * n + hf)
                                for h in range(HB):
                                    ins = E_.transpose(tp[:, h, :], prob[j % 2][:, HB * hf + h, :], m.ident[:])
                                ins.then_inc(S["turned"], 1)
                            pe.wait_ge(S["turned_kept"], 2 * n + 2)
                            weights = turned
                        else:
                            pe.wait_ge(S["shifted"], 2 * n + 2)
                            weights = prob[j % 2]
                        pe.wait_ge(S["v_kept"], g + 1)
                        pe.wait_ge(S["normed"], n)
                        for h in range(H):
                            ins = E_.matmul(read[:, h, :], weights[:, h, :], v1[:, j, h, :], start=True, stop=True)
                        ins.then_inc(S["read"], 1)
                        pe.wait_ge(S["normed"], n + 1)
                        pe.wait_ge(S["o_kept"], n)
                        E_.transpose(otp, o[:, j % 2, :], m.ident[:]).then_inc(S["o_turned"], 1)
                    pe.wait_ge(S["o_kept"], GB * (g + 1))
                    for j in range(GB):
                        c = slice(j * T, (j + 1) * T)
                        ins = E_.matmul(big[:, c], ot[:, c], w["o"][:], start=True, stop="o" not in bias)
                        if "o" in bias:
                            ins = E_.matmul(big[:, c], m.ones[0:1, 0:T], bias["o"][:], start=False, stop=True)
                    ins.then_inc(S["out_made"], 1)

            @block.scalar
            def _(act):
                act.wait_ge(S["ones_set"], 1)
                with A_.Fori(0, NG) as g:
                    if softmax:
                        act.wait_ge(S["q_made"], g + 1)
                        act.wait_ge(S["scores"], 2 * GB * g)
                        A_.mul(qt[:], big, HD ** -0.5).then_inc(S["q_kept"], 1)
                        act.wait_ge(S["k_made"], g + 1)
                        act.wait_ge(S["spread"], GB * g)
                        A_.copy(kt[:], big).then_inc(S["k_kept"], 1)
                    else:
                        act.wait_ge(S["q_low"], g + 1)
                        A_.activation(low[:, 0, :], low[:, 0, :], ACT.Exp).then_inc(S["q_exp"], 1)
                        act.wait_ge(S["k_low"], g + 1)
                        A_.activation(low[:, 1, :], low[:, 1, :], ACT.Exp).then_inc(S["k_exp"], 1)
                    act.wait_ge(S["v_made"], g + 1)
                    act.wait_ge(S["read"], GB * g)
                    A_.copy(v1[:, :, :, 0:HD], big.rearrange("p (j h d) -> p j h d", j=GB, d=HD)).then_inc(S["v_kept"], 1)
                    for j in range(GB):
                        n = g * GB + j
                        if softmax:
                            for hf in range(2):
                                act.wait_ge(S["shifted"], 2 * n + hf + 1)
                                h = slice(HB * hf, HB * hf + HB)
                                A_.activation(prob[j % 2][:, h, :], prob[j % 2][:, h, :], ACT.Exp).then_inc(S["weights"], 1)
                            for hf in range(2):
                                act.wait_ge(S["turned"], 2 * n + hf + 1)
                                if hf == 0:
                                    act.wait_ge(S["read"], n)
                                h = slice(HB * hf, HB * hf + HB)
                                A_.copy(turned[:, h, :], tp).then_inc(S["turned_kept"], 1)
                        act.wait_ge(S["o_turned"], n + 1)
                        act.wait_ge(S["out_made"], g)
                        A_.copy(ot[:, j * T:(j + 1) * T], otp).then_inc(S["o_kept"], 1)

            @block.vector
            def _(dve):
                V.memset(v1[:], 1.0).then_inc(S["ones_set"], 1)
                if mode == "masked":
                    dve.wait_ge(S["loaded"], n_load)
                    V.tensor_scalar(neg[:], mask_in[:], 0.0, -1e30, ALU.is_equal, ALU.mult).then_inc(S["masked"], 1)
                elif softmax:
                    dve.wait_ge(S["ones_set"], 1)
                    V.memset(top[:], 0.0).then_inc(S["masked"], 1)
                with V.Fori(0, NG) as g:
                    dchain.turn(0, g, 2 * GB)
                    if not softmax:
                        for i, (made, lowered, exped, kept, out) in enumerate((
                                ("q_made", "q_low", "q_exp", "q_kept", qt), ("k_made", "k_low", "k_exp", "k_kept", kt))):
                            dve.wait_ge(S[made], g + 1)
                            V.tensor_scalar(low[:, i, :], big, 0.0, None, ALU.min).then_inc(S[lowered], 1)
                            dve.wait_ge(S[exped], g + 1)
                            dve.wait_ge(S["spread"], GB * g)
                            dve.wait_ge(S["scores"], 2 * GB * g)
                            V.scalar_tensor_tensor(out=out[:], in0=big, scalar=0.0, in1=low[:, i, :], op0=ALU.max,
                                                   op1=ALU.add).then_inc(S[kept], 1)

                    def shift(j):
                        n = g * GB + j
                        for hf in range(2):
                            h = slice(HB * hf, HB * hf + HB)
                            dve.wait_ge(S["scores"], 2 * n + hf + 1)
                            if softmax:
                                V.tensor_reduce(top[:, j % 2, h], score(hf), AX.X, ALU.max).then_inc(S["max_taken"], 1)
                                dve.wait_ge(S["max_taken"], 2 * n + hf + 1)
                                dve.wait_ge(S["turned"], 2 * (g * GB + max(j - 1, 0)))
                                V.tensor_tensor(prob[j % 2][:, h, :], score(hf), over(top[:, j % 2, h].unsqueeze(2), 128, HB, T),
                                                ALU.subtract).then_inc(S["shifted"], 1)
                            else:
                                dve.wait_ge(S["read"], g * GB + max(j - 1, 0))
                                V.tensor_tensor(prob[j % 2][:, h, :], score(hf), over(m.causal[:].unsqueeze(1), 128, HB, T),
                                                ALU.mult).then_inc(S["shifted"], 1)

                    shift(0)
                    for j in range(GB):
                        n = g * GB + j
                        if j < GB - 1:
                            shift(j + 1)
                        dve.wait_ge(S["read"], n + 1)
                        dve.wait_ge(S["o_turned"], g * GB + max(j - 1, 0))
                        sums = read[:, :, HD:HD + 1].rearrange("p h o -> p (h o)")
                        dchain(dve, V.tensor_scalar(rec[:], sums, 0.0 if softmax else 1e-6, None, ALU.add))
                        dchain(dve, V.reciprocal(rec[:], rec[:]))
                        V.tensor_tensor(o[:, j % 2, :].rearrange("p (h d) -> p h d", d=HD), read[:, :, 0:HD],
                                        over(rec[:].unsqueeze(2), 128, H, HD), ALU.mult).then_inc(S["normed"], 1)
                    dve.wait_ge(S["out_made"], g + 1)
                    xs = target[:, bass.ts(g, GB), :]
                    V.tensor_tensor(xs, xs, big.rearrange("p (j d) -> p j d", d=D), ALU.add).then_inc(S["added"], 1)
                    assert dchain.n == 2 * GB
                dve.wait_ge(S["added"], NG)


E8, DFF = 8, 512
CHOSEN = NB * T * 2 // E8


def gate_logits(nc, m, st, S, w, b, logits):
    wg, bg = st.sb("wg", [128, E8]), st.sb("bg", [1, E8])
    rev = st.sb("rev", [128, E8])
    lp = m.ps[:, 0, 0:NB * E8].rearrange("p (b e) -> p b e", e=E8)

    def load(sp, a):
        sp.dma_start(wg[:], w).then_inc(S["loaded"], 16)
        sp.dma_start(rev[:], over(a["c_rev"].unsqueeze(0), 128, E8)).then_inc(S["loaded"], 16)
        if b is not None:
            sp.dma_start(bg[:], b.unsqueeze(0)).then_inc(S["loaded"], 16)

    def products(pe):
        pe.wait_ge(S["loaded"], 32 if b is None else 48)
        for i in range(NB):
            ins = nc.tensor.matmul(lp[:, i, :], m.xt[:, i * T:(i + 1) * T], wg[:], start=True, stop=b is None)
            if b is not None:
                ins = nc.tensor.matmul(lp[:, i, :], m.ones[0:1, 0:T], bg[:], start=False, stop=True)
        ins.then_inc(S["logits"], 1)
    return load, products, lp, rev


def first_best(nc, dve, chain, val, stat, work, rev, out):
    shape = [128, NB, E8]
    chain(dve, nc.vector.tensor_reduce(stat, val, AX.X, ALU.max))
    chain(dve, nc.vector.tensor_tensor(work, val, over(stat.unsqueeze(2), *shape), ALU.is_equal))
    chain(dve, nc.vector.tensor_tensor(work, work, over(rev[:].unsqueeze(1), *shape), ALU.mult))
    chain(dve, nc.vector.tensor_reduce(stat, work, AX.X, ALU.max))
    chain(dve, nc.vector.tensor_tensor(out, work, over(stat.unsqueeze(2), *shape), ALU.is_equal))


def softmax_experts(nc, dve, chain, S, logits, stat, shape):
    V = nc.vector
    chain(dve, V.tensor_reduce(stat, logits, AX.X, ALU.max))
    V.tensor_tensor(logits, logits, over(stat.unsqueeze(2), *shape), ALU.subtract).then_inc(S["shifted"], 1)
    dve.wait_ge(S["exped"], 1)
    chain(dve, V.tensor_reduce(stat, logits, AX.X, ALU.add))
    chain(dve, V.reciprocal(stat, stat))
    chain(dve, V.tensor_tensor(logits, logits, over(stat.unsqueeze(2), *shape), ALU.mult))


def softmax_exp(nc, S, logits):
    def program(act):
        act.wait_ge(S["shifted"], 1)
        nc.scalar.activation(logits, logits, ACT.Exp).then_inc(S["exped"], 1)
    return program


def route_one_stage(nc, m, a, comb):
    with Stage(nc, "r1") as st:
        S = {n: st.sem(n) for n in ("loaded", "logits")}
        chain = Chain(st.sem("dve_order"))
        val, work, stat = st.sb("val", [128, NB, E8]), st.sb("work", [128, NB, E8]), st.sb("stat", [128, NB])
        load, products, lp, rev = gate_logits(nc, m, st, S, a["L1_ffn_gate_W"], a["L1_ffn_gate_b"], val)
        with nc.Block() as block:
            block.sync(lambda sp: load(sp, a))
            block.tensor(products)

            @block.vector
            def _(dve):
                dve.wait_ge(S["logits"], 1)
                chain(dve, nc.vector.tensor_copy(val[:], lp))
                first_best(nc, dve, chain, val[:], stat[:], work[:], rev, comb[:])


def rank_tokens(nc, dve, chain, m, S, mask, totals, upto, turn):
    V = nc.vector
    dve.wait_ge(S["counted"], turn)
    within, whole = m.ps[:, 1, 0:E8 * NB], m.ps[:, 2, 0:E8 * NB]
    flat = lambda t: t.rearrange("p e b -> p (e b)")
    chain(dve, V.tensor_copy(flat(totals), whole))
    for e in range(E8):
        ins = V.tensor_tensor_scan(upto[:, e, :], m.ones[:, 0:NB], totals[:, e, :], 0.0, ALU.mult, ALU.add)
    chain(dve, ins)
    chain(dve, V.tensor_tensor(upto, upto, totals, ALU.subtract))
    chain(dve, V.tensor_tensor(flat(upto), flat(upto), within, ALU.add))


def count_tokens(nc, m, S, mask):
    flat = mask.rearrange("p e b -> p (e b)")
    nc.tensor.matmul(m.ps[:, 1, 0:E8 * NB], m.causal[:], flat, start=True, stop=True)
    nc.tensor.matmul(m.ps[:, 2, 0:E8 * NB], m.ones[:, 0:128], flat, start=True, stop=True).then_inc(S["counted"], 1)


def route_chosen_stage(nc, m, a, comb):
    BITS = range(29, -1, -1)
    with Stage(nc, "rk") as st:
        S = {n: st.sem(n) for n in ("loaded", "logits", "shifted", "exped", "tried", "taken", "counted")}
        chain = Chain(st.sem("dve_order"))
        val, stat = st.sb("val", [128, NB, E8]), st.sb("stat", [128, NB])
        score, work, tie, tot = (st.sb(n, [128, E8, NB]) for n in ("score", "work", "tie", "tot"))
        cur, cand = st.sb("cur", [128, E8], I32), st.sb("cand", [128, E8], I32)
        count, enough = st.sb("count", [128, E8]), st.sb("enough", [128, E8], I32)
        load, products, lp, rev = gate_logits(nc, m, st, S, a["L2_ffn_Wr"], None, val)
        V = nc.vector
        wide = lambda t: over(t.unsqueeze(2), 128, E8, NB)
        with nc.Block() as block:
            block.sync(lambda sp: load(sp, a))
            block.scalar(softmax_exp(nc, S, val[:]))

            @block.tensor
            def _(pe):
                products(pe)
                for i in range(len(BITS)):
                    pe.wait_ge(S["tried"], i + 1)
                    nc.tensor.matmul(m.ps[:, 3, 0:E8], m.ones[:, 0:128], count[:], start=True,
                                     stop=True).then_inc(S["taken"], 1)
                pe.wait_ge(S["tried"], len(BITS) + 1)
                nc.tensor.matmul(m.ps[:, 3, 0:E8], m.ones[:, 0:128], count[:], start=True,
                                 stop=True).then_inc(S["taken"], 1)
                count_tokens(nc, m, S, tie[:])

            @block.vector
            def _(dve):
                dve.wait_ge(S["logits"], 1)
                chain(dve, V.memset(cur[:], 0))
                chain(dve, V.tensor_copy(val[:], lp))
                softmax_experts(nc, dve, chain, S, val[:], stat[:], [128, NB, E8])
                chain(dve, V.tensor_copy(score[:], val[:].rearrange("p b e -> p e b")))
                for i, bit in enumerate(BITS):
                    chain(dve, V.tensor_scalar(cand[:], cur[:], 1 << bit, None, ALU.bitwise_or))
                    chain(dve, V.tensor_tensor(work[:], score[:], wide(cand[:].bitcast(F32)), ALU.is_ge))
                    V.tensor_reduce(count[:], work[:], AX.X, ALU.add).then_inc(S["tried"], 1)
                    dve.wait_ge(S["taken"], i + 1)
                    chain(dve, V.tensor_scalar(enough[:], m.ps[:, 3, 0:E8], float(CHOSEN), None, ALU.is_ge))
                    chain(dve, V.copy_predicated(cur[:], enough[:], cand[:]))
                last = cur[:].bitcast(F32)
                chain(dve, V.tensor_tensor(work[:], score[:], wide(last), ALU.is_gt))
                chain(dve, V.tensor_tensor(tie[:], score[:], wide(last), ALU.is_equal))
                V.tensor_reduce(count[:], work[:], AX.X, ALU.add).then_inc(S["tried"], 1)
                dve.wait_ge(S["taken"], len(BITS) + 1)
                chain(dve, V.tensor_scalar(count[:], m.ps[:, 3, 0:E8], -1.0, float(CHOSEN), ALU.mult, ALU.add))
                upto = val[:].rearrange("p b e -> p (b e)").rearrange("p (e b) -> p e b", b=NB)
                rank_tokens(nc, dve, chain, m, S, tie[:], tot[:], upto, 1)
                chain(dve, V.tensor_tensor(upto, upto, wide(count[:]), ALU.is_le))
                chain(dve, V.tensor_tensor(tie[:], tie[:], upto, ALU.mult))
                chain(dve, V.tensor_tensor(work[:], work[:], tie[:], ALU.add))
                chain(dve, V.tensor_tensor(comb[:].rearrange("p b e -> p e b"), work[:], score[:], ALU.mult))


def route_two_stage(nc, m, a, comb, place):
    with Stage(nc, "r2") as st:
        S = {n: st.sem(n) for n in ("loaded", "own_loaded", "logits", "shifted", "exped", "masked", "counted")}
        chain = Chain(st.sem("dve_order"))
        shape = [128, NB, E8]
        val, work, one, two = (st.sb(n, shape) for n in ("val", "work", "one", "two"))
        stat, own = st.sb("stat", [128, NB]), st.sb("own", [128, NB])
        mask, tot, upto, gap = (st.sb(n, [128, E8, NB]) for n in ("mask", "tot", "upto", "gap"))
        load, products, lp, rev = gate_logits(nc, m, st, S, a["L3_ffn_w_gate"], a["L3_ffn_b_gate"], val)
        V = nc.vector
        with nc.Block() as block:
            @block.sync
            def _(sp):
                load(sp, a)
                sp.dma_start(own[:], a["c_own"]).then_inc(S["own_loaded"], 16)

            block.scalar(softmax_exp(nc, S, val[:]))

            @block.tensor
            def _(pe):
                products(pe)
                pe.wait_ge(S["masked"], 1)
                count_tokens(nc, m, S, mask[:])

            @block.vector
            def _(dve):
                dve.wait_ge(S["own_loaded"], 16)
                dve.wait_ge(S["logits"], 1)
                chain(dve, V.tensor_copy(val[:], lp))
                softmax_experts(nc, dve, chain, S, val[:], stat[:], shape)
                first_best(nc, dve, chain, val[:], stat[:], work[:], rev, one[:])
                chain(dve, V.scalar_tensor_tensor(out=two[:], in0=one[:], scalar=-2.0, in1=val[:], op0=ALU.mult,
                                                  op1=ALU.add))
                chain(dve, V.tensor_copy(comb[:], two[:]))
                first_best(nc, dve, chain, comb[:], stat[:], work[:], rev, two[:])
                chain(dve, V.tensor_tensor(one[:], one[:], two[:], ALU.add))
                chain(dve, V.tensor_tensor(comb[:], one[:], val[:], ALU.mult))
                V.tensor_copy(mask[:], one[:].rearrange("p b e -> p e b")).then_inc(S["masked"], 1)
                dve.wait_ge(S["masked"], 1)
                rank_tokens(nc, dve, chain, m, S, mask[:], tot[:], upto[:], 1)
                bc = over(own[:].unsqueeze(1), 128, E8, NB)
                chain(dve, V.scalar_tensor_tensor(out=gap[:], in0=upto[:], scalar=-1.0, in1=bc, op0=ALU.add,
                                                  op1=ALU.subtract))
                chain(dve, V.tensor_tensor(gap[:], gap[:], mask[:], ALU.mult))
                chain(dve, V.tensor_tensor(place[:], gap[:], bc, ALU.add))


def experts_stage(nc, m, a, name, w1, b1, w2, b2, func, comb, target, place=None, rows=None, experts=E8):
    FC = DFF // 128
    scatter = place is not None
    with Stage(nc, name) as st:
        w1s, w2s = st.sb("w1", [128, experts, DFF]), st.sb("w2", [128, experts, FC, D])
        b1s, b2s = st.sb("b1", [128, experts, FC]), st.sb("b2", [1, experts, D])
        hid = [st.sb(f"hid{i}", [128, FC, GT]) for i in range(2)]
        term = [st.sb(f"term{i}", [128, GB, D]) for i in range(2)]
        idx = [st.sb(f"idx{i}", [128, GB], U32) for i in range(2)] if scatter else None
        zeros = st.sb("zeros", [128, 2048]) if scatter else None
        seen = st.sb("seen", [128, experts * NG]) if scatter else None
        S = {n: st.sem(n) for n in ("loaded", "up", "acted", "down", "weighed", "added", "cleared", "zeroed", "placed",
                                    "scattered0", "scattered1", "gathered")}
        V, A_, P_, E_ = nc.vector, nc.scalar, nc.gpsimd, nc.tensor
        ps = m.ps
        LOADED = 4 * 16
        HG = NG // 2
        with nc.Block() as block:
            @block.sync
            def _(sp):
                sp.dma_start(w1s[:], w1.rearrange("e d f -> d e f")).then_inc(S["loaded"], 16)
                sp.dma_start(b1s[:], b1).then_inc(S["loaded"], 16)
                sp.dma_start(w2s[:], w2.rearrange("e (c p) d -> p e c d", p=128)).then_inc(S["loaded"], 16)
                sp.dma_start(b2s[:], b2.unsqueeze(0)).then_inc(S["loaded"], 16)
                if scatter:
                    sp.wait_ge(S["cleared"], 1)
                    for i in range(4):
                        sp.dma_start(rows[2048 * i:2048 * (i + 1), :].rearrange("(p r) d -> p (r d)", p=128),
                                     zeros[:]).then_inc(S["zeroed"], 16)
                    sp.wait_ge(S["zeroed"], 64)
                    for i in range(2):
                        sp.wait_ge(S[f"scattered{i}"], 16 * GB * HG * experts)
                    sp.dma_start(m.xn[:], rows[0:NB * T, :].rearrange("(b t) d -> t b d", t=T)).then_inc(S["gathered"], 16)

            @block.tensor
            def _(pe):
                pe.wait_ge(S["loaded"], LOADED)
                for e in range(experts):
                    with E_.Fori(0, HG) as g2:
                        n0 = e * NG + g2 * 2
                        for i in range(2):
                            for c in range(FC):
                                pe.wait_ge(S["acted"], FC * (n0 + i - 1) + c + 1 if i else FC * n0)
                                E_.matmul(ps[:, c, :], w1s[:, e, c * 128:(c + 1) * 128],
                                          m.xt[:, bass.ds((g2 * 2 + i) * GT, GT)], start=True, stop=True).then_inc(S["up"], 1)
                        for i in range(2):
                            n = n0 + i
                            pe.wait_ge(S["acted"], FC * (n + 1))
                            pe.wait_ge(S["weighed"], n0)
                            for j in range(GB):
                                out = ps[:, 4 + i, j * D:(j + 1) * D]
                                for c in range(FC):
                                    E_.matmul(out, hid[i][:, c, j * T:(j + 1) * T], w2s[:, e, c, :], start=(c == 0), stop=False)
                                ins = E_.matmul(out, m.ones[0:1, 0:T], b2s[:, e, :], start=False, stop=True)
                            ins.then_inc(S["down"], 1)

            @block.scalar
            def _(act):
                act.wait_ge(S["loaded"], LOADED)
                for e in range(experts):
                    with A_.Fori(0, HG) as g2:
                        for i in range(2):
                            n = e * NG + g2 * 2 + i
                            for c in range(FC):
                                act.wait_ge(S["up"], FC * n + c + 1)
                                act.wait_ge(S["down"], e * NG + g2 * 2)
                                A_.activation(hid[i][:, c, :], ps[:, c, :], func, bias=b1s[:, e, c:c + 1]).then_inc(S["acted"], 1)

            @block.vector
            def _(dve):
                if scatter:
                    V.memset(zeros[:], 0.0).then_inc(S["cleared"], 1)
                for e in range(experts):
                    with V.Fori(0, HG) as g2:
                        for i in range(2):
                            n = e * NG + g2 * 2 + i
                            g = g2 * 2 + i
                            dve.wait_ge(S["down"], n + 1)
                            if scatter:
                                dve.wait_ge(S[f"scattered{i}"], 16 * GB * (e * HG + g2))
                                V.tensor_copy(idx[i][:], place[:, e, bass.ds(g * GB, GB)])
                            elif comb is not None:
                                dve.wait_ge(S["added"], e * NG + g2 * 2)
                            down = ps[:, 4 + i, :].rearrange("p (j d) -> p j d", d=D)
                            if comb is None:
                                xs = target[:, bass.ds(g * GB, GB), :]
                                V.tensor_tensor(xs, xs, down, ALU.add).then_inc(S["weighed"], 1)
                                continue
                            V.tensor_tensor(term[i][:], down,
                                            over(comb[:, bass.ds(g * GB, GB), e:e + 1], 128, GB, D),
                                            ALU.mult).then_inc(S["weighed"], 1)
                            if not scatter:
                                dve.wait_ge(S["weighed"], n + 1)
                                xs = target[:, bass.ds(g * GB, GB), :]
                                V.tensor_tensor(xs, xs, term[i][:], ALU.add).then_inc(S["added"], 1)
                if scatter:
                    dve.wait_ge(S["gathered"], 16)
                    V.tensor_tensor(target[:], target[:], m.xn[:], ALU.add).then_inc(S["added"], 1)
                    dve.wait_ge(S["added"], 1)
                else:
                    dve.wait_ge(S["added" if comb is not None else "weighed"], experts * NG)

            if scatter:
                @block.gpsimd
                def _(pool):
                    pool.wait_ge(S["zeroed"], 64)
                    for e in range(experts):
                        if e:
                            for i in range(2):
                                pool.wait_ge(S[f"scattered{i}"], 16 * GB * HG * e)
                        with P_.Fori(0, HG) as g2:
                            for i in range(2):
                                n = e * NG + g2 * 2 + i
                                pool.wait_ge(S["weighed"], n + 1)
                                P_.tensor_tensor(seen[:, bass.ds(n, 1)], m.ones[:, 0:1], m.ones[:, 0:1], ALU.mult)
                                for j in range(GB):
                                    P_.indirect_dma_start(
                                        rows, bass.IndirectOffsetOnAxis(ap=idx[i][:, j:j + 1], axis=0),
                                        term[i][:, j, :], None,
                                        compute_op=ALU.add).then_inc(S[f"scattered{i}"], 16)


def dense_softmax_stage(nc, m, a):
    with Stage(nc, "l2x") as st:
        S = {n: st.sem(n) for n in ("scores", "shifted", "weights", "turned", "turned_kept", "read", "added")}
        order = Chain(st.sem("dve_order"))
        top, sums = st.sb("top", [128, GB]), st.sb("sums", [128, GB])
        prob, pt, term = st.sb("prob", [128, GB, T]), st.sb("pt", [128, GB, T]), st.sb("term", [128, GB, D])
        V, A_, E_ = nc.vector, nc.scalar, nc.tensor
        bank = lambda g, k: m.ps[:, (g % 2) * 4 + k, :].rearrange("p (j t) -> p j t", t=T)
        with nc.Block() as block:
            @block.tensor
            def _(pe):
                def scores(g):
                    if g >= 2:
                        pe.wait_ge(S["added"], g - 1)
                    for j in range(GB):
                        c = slice((GB * g + j) * T, (GB * g + j + 1) * T)
                        ins = E_.matmul(bank(g, 0)[:, j, :], m.xt[:, c], m.ctxt[:, c], start=True, stop=True)
                    ins.then_inc(S["scores"], 1)

                scores(0)
                for g in range(NG):
                    if g < NG - 1:
                        scores(g + 1)
                    pe.wait_ge(S["weights"], g + 1)
                    for j in range(GB):
                        ins = E_.transpose(bank(g, 1)[:, j, :], prob[:, j, :], m.ident[:])
                    ins.then_inc(S["turned"], 1)
                    pe.wait_ge(S["turned_kept"], g + 1)
                    for j in range(GB):
                        ins = E_.matmul(bank(g, 2)[:, j, :], pt[:, j, :], m.ctx[:, GB * g + j, :], start=True, stop=True)
                    ins.then_inc(S["read"], 1)

            @block.scalar
            def _(act):
                for g in range(NG):
                    act.wait_ge(S["shifted"], g + 1)
                    A_.activation(prob[:], prob[:], ACT.Exp).then_inc(S["weights"], 1)
                    act.wait_ge(S["turned"], g + 1)
                    act.wait_ge(S["read"], g)
                    A_.copy(pt[:], bank(g, 1)).then_inc(S["turned_kept"], 1)

            @block.vector
            def _(dve):
                for g in range(NG):
                    dve.wait_ge(S["scores"], g + 1)
                    order(dve, V.tensor_reduce(top[:], bank(g, 0), AX.X, ALU.max))
                    dve.wait_ge(S["turned"], g)
                    V.tensor_tensor(prob[:], bank(g, 0), over(top[:].unsqueeze(2), 128, GB, T),
                                    ALU.subtract).then_inc(S["shifted"], 1)
                    dve.wait_ge(S["weights"], g + 1)
                    order(dve, V.tensor_reduce(sums[:], prob[:], AX.X, ALU.add))
                    order(dve, V.reciprocal(sums[:], sums[:]))
                    dve.wait_ge(S["read"], g + 1)
                    order(dve, V.tensor_tensor(term[:], bank(g, 2), over(sums[:].unsqueeze(2), 128, GB, D), ALU.mult))
                    xs = m.x[:, GB * g:GB * g + GB, :]
                    V.tensor_tensor(xs, xs, term[:], ALU.add).then_inc(S["added"], 1)
                dve.wait_ge(S["added"], NG)


def l1_ffn_stage(nc, m, a):
    with Stage(nc, "l1f") as st:
        comb = st.sb("comb", [128, NB, E8])
        route_one_stage(nc, m, a, comb)
        experts_stage(nc, m, a, "l1e", a["L1_ffn_W1"], a["L1_ffn_b1P"], a["L1_ffn_W2"], a["L1_ffn_b2"], ACT.Gelu, comb, m.x)


def l2_ffn_stage(nc, m, a):
    with Stage(nc, "l2f") as st:
        comb = st.sb("comb", [128, NB, E8])
        route_chosen_stage(nc, m, a, comb)
        experts_stage(nc, m, a, "l2e", a["L2_ffn_W1"], a["L2_ffn_b1P"], a["L2_ffn_W2"], a["L2_ffn_b2"], ACT.Gelu, comb, m.x)


def l2_attn_stage(nc, m, a):
    CH, NS, R = 256, 16, 64
    CC = CH // 128
    PROJ = R + 2 * NS
    with Stage(nc, "l2a") as st:
        w_in, w_out = st.sb("w_in", [128, 2 * CH]), st.sb("w_out", [128, CC, D])
        w_x, w_dt = st.sb("w_x", [128, CC, PROJ]), st.sb("w_dt", [R, CH])
        taps, cb, dtb, skip = (st.sb(n, [128, CC, k]) for n, k in (("taps", 4), ("cb", 1), ("dtb", 1), ("skip", 1)))
        rate, ln_w, pick = st.sb("rate", [128, CC, NS]), st.sb("ln_w", [128, PROJ]), st.sb("pick", [NS, NS, 128])
        cin = st.sb("cin", [128, CC, GB, T + 3])
        u, gate, ta = (st.sb(n, [128, CC, GB, T]) for n in ("u", "gate", "ta"))
        sq, xdbl = st.sb("sq", [128, GB, PROJ]), st.sb("xdbl", [128, GB, PROJ])
        mean, root = st.sb("mean", [128, GB, 3]), st.sb("root", [128, GB, 3])
        dtt, bt, ct = st.sb("dtt", [R, GT]), st.sb("bt", [NS, GT]), st.sb("ct", [NS, GT])
        dt, sg, one, du, y = (st.sb(n, [128, CC, GT]) for n in ("dt", "sg", "one", "du", "y"))
        decay = [st.sb(f"decay{i}", [128, GB, T]) for i in range(4)]
        push = [st.sb(f"push{i}", [128, GT]) for i in range(2)]
        state = [st.sb(f"state{i}", [128, GT]) for i in range(2)]
        read = [st.sb(f"read{i}", [128, GT]) for i in range(2)]
        xg = st.sb("xg", [128, GT])
        S = {n: st.sem(n) for n in (
            "loaded", "cleared", "rates", "hs_made", "conv_in", "conv_out", "u_ready", "gate_ready", "x_made", "x_squared",
            "mean_ready", "rooted", "x_normed", "x_turned", "x_kept", "dt_made", "dt_low", "dt_exp", "dt_one", "dt_log",
            "pushes", "b_spread", "decays", "pushed", "scanned", "read", "summed", "y_gated", "out_made", "added")}
        dchain, pchain = Chain(st.sem("dve_order")), Chain(st.sem("pool_order"))
        V, A_, P_, E_ = nc.vector, nc.scalar, nc.gpsimd, nc.tensor
        ps = m.ps
        g4 = lambda t: t.rearrange("p (b t) -> p b t", t=T)
        c4 = lambda t: t.rearrange("p c (b t) -> p c b t", t=T)
        xp = ps[:, 4, 0:GB * PROJ].rearrange("p (b k) -> p b k", k=PROJ)
        parts = ((0, R), (R, NS), (R + NS, NS))
        loads = ((w_in, "L2_attn_in_proj_wT", None), (w_out, "L2_attn_out_proj_wT", "(c p) n -> p c n"),
                 (w_x, "L2_attn_x_proj_wT", "(c p) n -> p c n"), (w_dt, "L2_attn_dt_proj_wT", None),
                 (taps, "L2_attn_conv_w", "(c p) o k -> p c (o k)"), (cb, "L2_attn_conv_bP", None),
                 (dtb, "L2_attn_dt_proj_bP", None), (skip, "L2_attn_DP", None),
                 (rate, "L2_attn_A_log", "(c p) n -> p c n"), (pick, "c_pick", None))
        LOADED = 16 * (len(loads) + 3)
        with nc.Block() as block:
            @block.sync
            def _(sp):
                for dst, src, how in loads:
                    s = a[src]
                    if how:
                        s = s.rearrange(how, p=128)
                    sp.dma_start(dst[:], s).then_inc(S["loaded"], 16)
                for (c0, n), src in zip(parts, ("L2_attn_dt_ln_w", "L2_attn_b_ln_w", "L2_attn_c_ln_w")):
                    sp.dma_start(ln_w[:, c0:c0 + n], over(a[src].unsqueeze(0), 128, n)).then_inc(S["loaded"], 16)

            @block.tensor
            def _(pe):
                pe.wait_ge(S["loaded"], LOADED)
                with E_.Fori(0, NG) as g:
                    pe.wait_ge(S["added"], g)
                    for c in range(2 * CC):
                        E_.matmul(ps[:, c, :], w_in[:, c * 128:(c + 1) * 128], m.xt[:, bass.ts(g, GT)], start=True,
                                  stop=True).then_inc(S["hs_made"], 1)
                    pe.wait_ge(S["u_ready"], g + 1)
                    for j in range(GB):
                        for c in range(CC):
                            ins = E_.matmul(xp[:, j, :], u[:, c, j, :], w_x[:, c, :], start=(c == 0), stop=(c == CC - 1))
                    ins.then_inc(S["x_made"], 1)
                    pe.wait_ge(S["x_normed"], g + 1)
                    for k in (1, 2, 0):
                        c0, n = parts[k]
                        for j in range(GB):
                            ins = E_.transpose(ps[0:n, 5 + k, j * T:(j + 1) * T], xdbl[:, j, c0:c0 + n], m.ident[:])
                    ins.then_inc(S["x_turned"], 1)
                    pe.wait_ge(S["x_kept"], g + 1)
                    for c in range(CC):
                        ins = E_.matmul(ps[:, c, :], w_dt[:, c * 128:(c + 1) * 128], dtt[:], start=True, stop=True)
                    ins.then_inc(S["dt_made"], 1)
                    for n in range(NS):
                        if n >= 2:
                            pe.wait_ge(S["read"], CC * (g * NS + n - 1))
                        b = 4 + 2 * (n % 2)
                        E_.matmul(ps[:, b, :], pick[:, n, :], bt[:], start=True, stop=True)
                        E_.matmul(ps[:, b + 1, :], pick[:, n, :], ct[:], start=True, stop=True).then_inc(S["b_spread"], 1)
                    pe.wait_ge(S["y_gated"], g + 1)
                    for j in range(GB):
                        for c in range(CC):
                            ins = E_.matmul(ps[:, 2, j * D:(j + 1) * D], y[:, c, j * T:(j + 1) * T], w_out[:, c, :],
                                            start=(c == 0), stop=(c == CC - 1))
                    ins.then_inc(S["out_made"], 1)

            @block.scalar
            def _(act):
                act.wait_ge(S["loaded"], LOADED)
                act.wait_ge(S["cleared"], 1)
                A_.activation(rate[:], rate[:], ACT.Exp).then_inc(S["rates"], 1)
                act.wait_ge(S["rates"], 2)
                with A_.Fori(0, NG) as g:
                    for c in range(CC):
                        act.wait_ge(S["hs_made"], 2 * CC * g + c + 1)
                        A_.copy(cin[:, c, :, 1:1 + T], g4(ps[:, c, :])).then_inc(S["conv_in"], 1)
                    for c in range(CC):
                        act.wait_ge(S["hs_made"], 2 * CC * g + CC + c + 1)
                        ins = A_.activation(gate[:, c, :, :], g4(ps[:, CC + c, :]), ACT.Silu)
                    ins.then_inc(S["gate_ready"], 1)
                    act.wait_ge(S["conv_out"], g + 1)
                    for c in range(CC):
                        ins = A_.activation(u[:, c], u[:, c], ACT.Silu, bias=cb[:, c, :])
                    ins.then_inc(S["u_ready"], 1)
                    act.wait_ge(S["x_made"], g + 1)
                    A_.activation(sq[:], xp, ACT.Square).then_inc(S["x_squared"], 1)
                    act.wait_ge(S["mean_ready"], g + 1)
                    A_.activation(root[:], mean[:], ACT.Sqrt).then_inc(S["rooted"], 1)
                    act.wait_ge(S["x_turned"], g + 1)
                    A_.copy(dtt[:], ps[0:R, 5, :])
                    A_.copy(bt[:], ps[0:NS, 6, :])
                    A_.copy(ct[:], ps[0:NS, 7, :]).then_inc(S["x_kept"], 1)
                    act.wait_ge(S["dt_low"], g + 1)
                    A_.activation(sg[:], sg[:], ACT.Exp).then_inc(S["dt_exp"], 1)
                    act.wait_ge(S["dt_one"], g + 1)
                    A_.activation(du[:], one[:], ACT.Ln).then_inc(S["dt_log"], 1)
                    act.wait_ge(S["pushes"], g + 1)
                    for n in range(NS):
                        for c in range(CC):
                            k = CC * n + c
                            if k >= 4:
                                act.wait_ge(S["scanned"], g * NS * CC + k - 3)
                            A_.activation(decay[k % 4][:, :, 1:T], c4(dt[:])[:, c, :, 1:T], ACT.Exp,
                                          scale=rate[:, c, n:n + 1]).then_inc(S["decays"], 1)

            @block.gpsimd
            def _(pool):
                with P_.Fori(0, NG) as g:
                    pchain.turn(0, g, (NS - 1) * CC)
                    for n in range(NS):
                        for c in range(CC):
                            k = CC * n + c
                            pool.wait_ge(S["read"], g * NS * CC + k + 1)
                            if n == 0:
                                pool.wait_ge(S["out_made"], g)
                                P_.tensor_tensor(y[:, c, :], read[k % 2][:], m.ones[:], ALU.mult).then_inc(S["summed"], 1)
                            else:
                                pool.wait_ge(S["summed"], g * NS * CC + k - 1)
                                P_.tensor_tensor(y[:, c, :], y[:, c, :], read[k % 2][:], ALU.add).then_inc(S["summed"], 1)

            @block.vector
            def _(dve):
                ins = V.memset(cin[:], 0.0)
                for i in range(4):
                    ins = V.memset(decay[i][:], 0.0)
                ins.then_inc(S["cleared"], 1)
                dve.wait_ge(S["rates"], 1)
                V.tensor_scalar(rate[:], rate[:], -1.0, None, ALU.mult).then_inc(S["rates"], 1)
                per = CC * 4 + 3 + 6 + 2
                with V.Fori(0, NG) as g:
                    dchain.turn(0, g, per)
                    dve.wait_ge(S["conv_in"], CC * (g + 1))
                    dve.wait_ge(S["out_made"], g)
                    for c in range(CC):
                        tap = lambda k: taps[:, c, k:k + 1]
                        dchain(dve, V.tensor_scalar(u[:, c], cin[:, c, :, 0:T], tap(0), None, ALU.mult))
                        for k in range(1, 4):
                            dchain(dve, V.scalar_tensor_tensor(out=u[:, c], in0=cin[:, c, :, k:k + T], scalar=tap(k),
                                                               in1=u[:, c], op0=ALU.mult, op1=ALU.add))
                    V.tensor_copy(mean[:, 0, 0:1], taps[:, 0, 0:1]).then_inc(S["conv_out"], 1)
                    dve.wait_ge(S["conv_out"], g + 1)
                    dve.wait_ge(S["x_squared"], g + 1)
                    for k, (c0, n) in enumerate(parts):
                        ins = V.tensor_reduce(mean[:, :, k:k + 1], sq[:, :, c0:c0 + n], AX.X, ALU.add)
                    dchain(dve, ins)
                    for k, (c0, n) in enumerate(parts):
                        ins = V.tensor_scalar(mean[:, :, k:k + 1], mean[:, :, k:k + 1], 1.0 / n, 1e-6, ALU.mult, ALU.add)
                    ins.then_inc(S["mean_ready"], 1)
                    dve.wait_ge(S["rooted"], g + 1)
                    dchain(dve, V.reciprocal(mean[:], root[:]))
                    for k, (c0, n) in enumerate(parts):
                        ins = V.tensor_tensor(xdbl[:, :, c0:c0 + n], xp[:, :, c0:c0 + n],
                                              over(mean[:, :, k:k + 1], 128, GB, n), ALU.mult)
                    dchain(dve, ins)
                    V.tensor_tensor(xdbl[:], xdbl[:], over(ln_w[:].unsqueeze(1), 128, GB, PROJ),
                                    ALU.mult).then_inc(S["x_normed"], 1)
                    dve.wait_ge(S["dt_made"], g + 1)
                    dchain(dve, V.tensor_tensor(dt[:], ps[:, 0:CC, :], over(dtb[:], 128, CC, GT), ALU.add))
                    V.scalar_tensor_tensor(out=sg[:], in0=dt[:], scalar=-1.0, in1=dt[:], op0=ALU.mult,
                                           op1=ALU.min).then_inc(S["dt_low"], 1)
                    dve.wait_ge(S["dt_exp"], g + 1)
                    V.tensor_scalar(one[:], sg[:], 1.0, None, ALU.add).then_inc(S["dt_one"], 1)
                    dve.wait_ge(S["dt_log"], g + 1)
                    tf = ta[:].rearrange("p c b t -> p c (b t)")
                    dchain(dve, V.tensor_scalar(tf, one[:], 1.0, 1e-30, ALU.subtract, ALU.max))
                    dchain(dve, V.reciprocal(tf, tf))
                    dchain(dve, V.tensor_tensor(du[:], du[:], sg[:], ALU.mult))
                    V.scalar_tensor_tensor(out=one[:], in0=one[:], scalar=1.0, in1=sg[:], op0=ALU.is_equal, op1=ALU.mult)
                    dchain(dve, V.tensor_tensor(du[:], du[:], tf, ALU.mult))
                    dchain(dve, V.tensor_tensor(du[:], du[:], one[:], ALU.add))
                    dchain(dve, V.scalar_tensor_tensor(out=dt[:], in0=dt[:], scalar=0.0, in1=du[:], op0=ALU.max,
                                                       op1=ALU.add))
                    V.tensor_tensor(c4(du[:]), c4(dt[:]), u[:], ALU.mult).then_inc(S["pushes"], 1)
                    dve.wait_ge(S["pushes"], g + 1)
                    for n in range(NS):
                        dve.wait_ge(S["b_spread"], g * NS + n + 1)
                        b = 4 + 2 * (n % 2)
                        for c in range(CC):
                            k = CC * n + c
                            V.tensor_tensor(push[c][:], du[:, c, :], ps[:, b, :], ALU.mult).then_inc(S["pushed"], 1)
                        for c in range(CC):
                            k = CC * n + c
                            dve.wait_ge(S["pushed"], g * NS * CC + k + 1)
                            dve.wait_ge(S["decays"], g * NS * CC + k + 1)
                            V.tensor_tensor_scan(state[c][:], decay[k % 4][:].rearrange("p b t -> p (b t)"), push[c][:],
                                                 0.0, ALU.mult, ALU.add).then_inc(S["scanned"], 1)
                        for c in range(CC):
                            k = CC * n + c
                            dve.wait_ge(S["scanned"], g * NS * CC + k + 1)
                            dve.wait_ge(S["summed"], g * NS * CC + max(k - 1, 0))
                            V.tensor_tensor(read[c][:], state[c][:], ps[:, b + 1, :], ALU.mult).then_inc(S["read"], 1)
                    dve.wait_ge(S["summed"], NS * CC * (g + 1))
                    dve.wait_ge(S["gate_ready"], g + 1)
                    for c in range(CC):
                        ins = V.scalar_tensor_tensor(out=g4(y[:, c, :]), in0=u[:, c], scalar=skip[:, c, :],
                                                     in1=g4(y[:, c, :]), op0=ALU.mult, op1=ALU.add)
                    dchain(dve, ins)
                    V.tensor_tensor(c4(y[:]), c4(y[:]), gate[:], ALU.mult).then_inc(S["y_gated"], 1)
                    dve.wait_ge(S["out_made"], g + 1)
                    xs = m.x[:, bass.ts(g, GB), :]
                    V.tensor_tensor(xs, xs, ps[:, 2, :].rearrange("p (j d) -> p j d", d=D), ALU.add).then_inc(S["added"], 1)
                dve.wait_ge(S["added"], NG)


def l3_xattn_stage(nc, m, a, feat):
    with Stage(nc, "l3x") as st:
        S = {n: st.sem(n) for n in (
            "loaded", "squashed", "probs", "logs", "diffs", "turned", "kept", "scores", "shifted", "weights",
            "w_turned", "w_kept", "read", "diff", "d_turned", "d_kept", "out", "done")}
        order = Chain(st.sem("dve_order"))
        w, b = st.sb("w", [128, D]), st.sb("b", [1, GB, D])
        full = [128, NB, D]
        pa, pb = st.sb("pa", full), st.sb("pb", full)
        sums = st.sb("sums", [128, 2, NB])
        lrt = st.sb("lrt", [128, NB * T])
        top, tot = st.sb("top", [128, GB]), st.sb("tot", [128, GB])
        prob, pt, diff = st.sb("prob", [128, GB, T]), st.sb("pt", [128, GB, T]), st.sb("diff", [128, GB, D])
        dt = st.sb("dt", [128, GB, T])
        V, A_, E_ = nc.vector, nc.scalar, nc.tensor
        bank = lambda g, k: m.ps[:, (g % 2) * 4 + k, :].rearrange("p (j t) -> p j t", t=T)
        with nc.Block() as block:
            @block.sync
            def _(sp):
                sp.dma_start(w[:], a["L3_xattn_W_diffT"]).then_inc(S["loaded"], 16)
                sp.dma_start(b[:], over(a["L3_xattn_b_diff"].unsqueeze(0).unsqueeze(0), 1, GB, D)).then_inc(S["loaded"], 16)

            @block.scalar
            def _(act):
                A_.activation(pa[:], m.xn[:], ACT.Tanh).then_inc(S["squashed"], 1)
                A_.activation(pb[:], m.ctx[:], ACT.Tanh).then_inc(S["squashed"], 1)
                act.wait_ge(S["probs"], 2)
                A_.activation(feat[:], pb[:], ACT.Ln).then_inc(S["logs"], 1)
                act.wait_ge(S["diffs"], 1)
                A_.activation(pb[:], pa[:], ACT.Ln).then_inc(S["logs"], 1)
                for k in range(2):
                    for g in range(0, NG, 2):
                        act.wait_ge(S["turned"], k * NG + g + 1)
                        dst = (m.xt, lrt)[k]
                        A_.copy(dst[:, g * GT:(g + 1) * GT], m.ps[:, g, :]).then_inc(S["kept"], 1)
                for g in range(NG):
                    act.wait_ge(S["shifted"], g + 1)
                    A_.activation(prob[:], prob[:], ACT.Exp, scale=-D ** -0.5).then_inc(S["weights"], 1)
                    act.wait_ge(S["w_turned"], g + 1)
                    A_.copy(pt[:], bank(g, 1)).then_inc(S["w_kept"], 1)
                    act.wait_ge(S["d_turned"], g + 1)
                    A_.copy(dt[:], bank(g, 3)).then_inc(S["d_kept"], 1)

            @block.vector
            def _(dve):
                wide = lambda i: over(sums[:, i, :].unsqueeze(2), *full)
                for i, p in enumerate((pa, pb)):
                    dve.wait_ge(S["squashed"], i + 1)
                    order(dve, V.tensor_scalar(p[:], p[:], 0.499, 0.5, ALU.mult, ALU.add))
                    order(dve, V.tensor_reduce(sums[:, i, :], p[:], AX.X, ALU.add))
                    order(dve, V.tensor_scalar(sums[:, i, :], sums[:, i, :], 1e-8, None, ALU.add))
                    order(dve, V.reciprocal(sums[:, i, :], sums[:, i, :]))
                    order(dve, V.tensor_tensor(p[:], p[:], wide(i), ALU.mult))
                    V.tensor_scalar(p[:], p[:], 1e-8, None, ALU.max).then_inc(S["probs"], 1)
                dve.wait_ge(S["logs"], 1)
                order(dve, V.tensor_tensor(lrt[:].rearrange("p (b d) -> p b d", d=D), pa[:], pb[:], ALU.subtract))
                V.tensor_copy(sums[:, 0, 0:1], sums[:, 1, 0:1]).then_inc(S["diffs"], 1)
                dve.wait_ge(S["logs"], 2)
                order(dve, V.tensor_tensor(pb[:], pb[:], feat[:], ALU.subtract))
                V.tensor_copy(pa[:], lrt[:].rearrange("p (b d) -> p b d", d=D)).then_inc(S["diffs"], 1)
                for k in range(2):
                    for g in range(1, NG, 2):
                        dve.wait_ge(S["turned"], k * NG + g + 1)
                        dst = (m.xt, lrt)[k]
                        V.tensor_copy(dst[:, g * GT:(g + 1) * GT], m.ps[:, g, :]).then_inc(S["kept"], 1)
                for g in range(NG):
                    s = slice(GB * g, GB * g + GB)
                    dve.wait_ge(S["scores"], g + 1)
                    order(dve, V.tensor_reduce(top[:], bank(g, 0), AX.X, ALU.min))
                    dve.wait_ge(S["w_turned"], g)
                    V.tensor_tensor(prob[:], bank(g, 0), over(top[:].unsqueeze(2), 128, GB, T), ALU.subtract).then_inc(S["shifted"], 1)
                    dve.wait_ge(S["weights"], g + 1)
                    order(dve, V.tensor_reduce(tot[:], prob[:], AX.X, ALU.add))
                    order(dve, V.reciprocal(tot[:], tot[:]))
                    dve.wait_ge(S["read"], g + 1)
                    dve.wait_ge(S["d_turned"], g)
                    order(dve, V.tensor_tensor(diff[:], bank(g, 2), over(tot[:].unsqueeze(2), 128, GB, D), ALU.mult))
                    V.tensor_tensor(diff[:], m.ctx[:, s, :], diff[:], ALU.subtract).then_inc(S["diff"], 1)
                    dve.wait_ge(S["out"], g + 1)
                    V.tensor_tensor(feat[:, s, :], m.xn[:, s, :], bank(g, 2), ALU.add).then_inc(S["done"], 1)
                dve.wait_ge(S["done"], NG)

            @block.tensor
            def _(pe):
                pe.wait_ge(S["diffs"], 2)
                for k, src in enumerate((pa, pb)):
                    for g in range(NG):
                        if k:
                            pe.wait_ge(S["kept"], NG)
                        for j in range(GB):
                            ins = E_.transpose(m.ps[:, g, j * T:(j + 1) * T], src[:, GB * g + j, :], m.ident[:])
                        ins.then_inc(S["turned"], 1)
                pe.wait_ge(S["kept"], 2 * NG)
                pe.wait_ge(S["loaded"], 32)

                def scores(g):
                    if g >= 2:
                        pe.wait_ge(S["done"], g - 1)
                    for j in range(GB):
                        c = slice((GB * g + j) * T, (GB * g + j + 1) * T)
                        ins = E_.matmul(bank(g, 0)[:, j, :], m.xt[:, c], lrt[:, c], start=True, stop=True)
                    ins.then_inc(S["scores"], 1)

                scores(0)
                for g in range(NG):
                    if g < NG - 1:
                        scores(g + 1)
                    pe.wait_ge(S["weights"], g + 1)
                    for j in range(GB):
                        ins = E_.transpose(bank(g, 1)[:, j, :], prob[:, j, :], m.ident[:])
                    ins.then_inc(S["w_turned"], 1)
                    pe.wait_ge(S["w_kept"], g + 1)
                    for j in range(GB):
                        ins = E_.matmul(bank(g, 2)[:, j, :], pt[:, j, :], m.ctx[:, GB * g + j, :], start=True, stop=True)
                    ins.then_inc(S["read"], 1)
                    pe.wait_ge(S["diff"], g + 1)
                    for j in range(GB):
                        ins = E_.transpose(bank(g, 3)[:, j, :], diff[:, j, :], m.ident[:])
                    ins.then_inc(S["d_turned"], 1)
                    pe.wait_ge(S["d_kept"], g + 1)
                    for j in range(GB):
                        E_.matmul(bank(g, 2)[:, j, :], dt[:, j, :], w[:], start=True, stop=False)
                        ins = E_.matmul(bank(g, 2)[:, j, :], m.ones[0:1, 0:T], b[:, j, :], start=False, stop=True)
                    ins.then_inc(S["out"], 1)


def merge_stage(nc, m, name, dst, src, add):
    with Stage(nc, name) as st:
        merged = st.sem("merged")
        with nc.Block() as block:
            @block.vector
            def _(dve):
                if add:
                    nc.vector.tensor_tensor(dst[:], dst[:], src[:], ALU.add).then_inc(merged, 1)
                else:
                    nc.vector.tensor_copy(dst[:], src[:]).then_inc(merged, 1)
                dve.wait_ge(merged, 1)


def l3_cross_stage(nc, m, a):
    with Stage(nc, "l3c") as st:
        feat = st.sb("feat", [128, NB, D])
        affine = (a["L3_xattn_ln_g"], a["L3_xattn_ln_b"])
        l3_xattn_stage(nc, m, a, feat)
        norm_stage(nc, m, "n10a", src=feat, affine=affine)
        experts_stage(nc, m, a, "l3m", a["L3_xattn_W1T"], a["L3_xattn_b1P"], a["L3_xattn_W2T"], a["L3_xattn_b2P"], ACT.Gelu,
                      None, feat, experts=1)
        norm_stage(nc, m, "n10b", False, src=feat, affine=affine)
        merge_stage(nc, m, "l3s", m.x, m.xn, True)


def l3_ffn_stage(nc, m, a):
    with Stage(nc, "l3f") as st:
        y = m.ctx
        merge_stage(nc, m, "l3y", y, m.xn, False)
        norm_stage(nc, m, "n11a", src=y, affine=(a["L3_ffn_ln1_scale"], a["L3_ffn_ln1_bias"]))
        w, b = a["L3_ffn_w_qkv"], a["L3_ffn_b_qkv"]
        head_attn_stage(nc, m, a, "l3h", "causal", w[:, 0:D], w[:, D:2 * D], w[:, 2 * D:3 * D], a["L3_ffn_w_attnproj"],
                        m.xt, y, b[0:D], b[D:2 * D], b[2 * D:3 * D], a["L3_ffn_b_attnproj"])
        norm_stage(nc, m, "n11b", src=y, affine=(a["L3_ffn_ln2_scale"], a["L3_ffn_ln2_bias"]))
        comb, place = st.sb("comb", [128, NB, E8]), st.sb("place", [128, E8, NB])
        route_two_stage(nc, m, a, comb, place)
        rows = nc.dram_tensor("expert_rows", (2 * NB * T, D), F32, kind="Internal").ap()
        experts_stage(nc, m, a, "l3e", a["L3_ffn_w_fc"], a["L3_ffn_b_fcP"], a["L3_ffn_w_fcproj"], a["L3_ffn_b_fcproj"],
                      ACT.Gelu_apprx_tanh, comb, y, place, rows)
        merge_stage(nc, m, "l3z", m.x, y, True)


class Shared:

    def __init__(self, nc, stack):
        sb = lambda n, s, dt=F32: stack.enter_context(nc.sbuf_tensor(n, s, dt))
        self.x, self.xn = sb("x_res", [128, NB, D]), sb("x_norm", [128, NB, D])
        self.xt = sb("x_norm_t", [128, NB * T])
        self.ctx, self.ctxt = sb("ctx_tok", [128, NB, D]), sb("ctx_feat", [128, NB * T])
        self.ident, self.causal = sb("ident", [128, 128]), sb("causal", [128, 128])
        self.heads, self.ones = sb("heads", [128, 128]), sb("ones", [128, GT])
        self.ps = stack.enter_context(nc.psum_tensor("banks", [128, 8, 512], F32))


def store_stage(nc, m, a):
    with Stage(nc, "store") as st:
        stored = st.sem("stored")
        with nc.Block() as block:
            @block.sync
            def _(sp):
                sp.dma_start(a["out"].rearrange("b t d -> t b d"), m.x[:]).then_inc(stored, 16)
                sp.wait_ge(stored, 16)


STAGES = [
    lambda nc, m, a: (norm_stage(nc, m, "n0"), l0_attn_stage(nc, m, a)),
    lambda nc, m, a: (norm_stage(nc, m, "n1", False), l0_xattn_stage(nc, m, a)),
    lambda nc, m, a: (norm_stage(nc, m, "n2", False), l0_ffn_stage(nc, m, a)),
    lambda nc, m, a: (norm_stage(nc, m, "n3"), l1_attn_stage(nc, m, a)),
    lambda nc, m, a: (norm_stage(nc, m, "n4"), head_attn_stage(
        nc, m, a, "l1x", "masked", a["L1_xattn_Wq"], a["L1_xattn_Wk"], a["L1_xattn_Wv"], a["L1_xattn_Wo"], m.ctxt, m.x,
        a["L1_xattn_bq"], a["L1_xattn_bk"], a["L1_xattn_bv"], a["L1_xattn_bo"])),
    lambda nc, m, a: (norm_stage(nc, m, "n5"), l1_ffn_stage(nc, m, a)),
    lambda nc, m, a: (norm_stage(nc, m, "n6"), l2_attn_stage(nc, m, a)),
    lambda nc, m, a: (norm_stage(nc, m, "n7"), dense_softmax_stage(nc, m, a)),
    lambda nc, m, a: (norm_stage(nc, m, "n8"), l2_ffn_stage(nc, m, a)),
    lambda nc, m, a: (norm_stage(nc, m, "n9"), head_attn_stage(
        nc, m, a, "l3a", "linear", a["L3_attn_w_attn"][:, 0:D], a["L3_attn_w_attn"][:, D:2 * D],
        a["L3_attn_w_attn"][:, 2 * D:3 * D], a["L3_attn_w_proj"], m.xt, m.x)),
    lambda nc, m, a: (norm_stage(nc, m, "n10", False), l3_cross_stage(nc, m, a)),
    lambda nc, m, a: (norm_stage(nc, m, "n11", False), l3_ffn_stage(nc, m, a)),
]


def decoder(nc, a, stages=STAGES):
    with ExitStack() as stack:
        m = Shared(nc, stack)
        load_stage(nc, m, a)
        for stage in stages:
            stage(nc, m, a)
        store_stage(nc, m, a)


def constants():
    s, t = np.arange(T)[:, None], np.arange(T)[None, :]
    f = np.float32
    return {
        "c_ident": np.eye(128, dtype=f),
        "c_ones": np.ones((128, GT), f),
        "c_causal": (s <= t).astype(f),
        "c_heads": (s // HD == t // HD).astype(f),
        "c_hmask": (np.arange(128)[:, None] // HD == np.arange(H)[None, :]).astype(f),
        "c_future": np.where(t > s, -1e30, 0).astype(f),
        "c_rev": np.arange(E8, 0, -1).astype(f),
        "c_own": (NB * T + np.arange(NB)[None, :] * T + s).astype(f),
        "c_pick": np.repeat(np.eye(16, dtype=f)[:, :, None], 128, 2),
        "c_strict": (s > t).astype(f),
        "c_levels": np.stack([(s >> l + 1 == t >> l + 1) & (s >> l & 1 == 0) & (t >> l & 1 == 1)
                              for l in range(LEVELS)], 1).astype(f),
        "c_pair": np.stack([np.arange(128) < 64, np.arange(128) >= 64], 1).astype(f),
    }


def arrange(inputs):
    arrays = {k: np.ascontiguousarray(v) for k, v in inputs.items()}
    for n in ("L3_xattn_W_diff", "L2_attn_in_proj_w", "L2_attn_out_proj_w", "L2_attn_x_proj_w", "L2_attn_dt_proj_w", "L0_attn_Wq", "L0_attn_Wk", "L0_attn_Wv", "L0_attn_Wo"):
        arrays[n + "T"] = np.ascontiguousarray(np.transpose(arrays.pop(n)))
    for n in ("L1_ffn_b1", "L2_ffn_b1", "L3_ffn_b_fc"):
        v = arrays.pop(n)
        arrays[n + "P"] = np.ascontiguousarray(v.reshape(E8, DFF // 128, 128).transpose(2, 0, 1))
    for n in ("L2_attn_conv_b", "L2_attn_dt_proj_b", "L2_attn_D"):
        arrays[n + "P"] = np.ascontiguousarray(arrays.pop(n).reshape(2, 128, 1).transpose(1, 0, 2))
    arrays["L3_xattn_W1T"] = np.ascontiguousarray(arrays.pop("L3_xattn_W1").T)[None]
    arrays["L3_xattn_W2T"] = np.ascontiguousarray(arrays.pop("L3_xattn_W2").T)[None]
    arrays["L3_xattn_b1P"] = np.ascontiguousarray(arrays.pop("L3_xattn_b1").reshape(1, DFF // 128, 128).transpose(2, 0, 1))
    arrays["L3_xattn_b2P"] = arrays.pop("L3_xattn_b2")[None]
    arrays.update(constants())
    return arrays


def kernel(**inputs):
    import concourse.bacc as bacc
    from concourse.bass_utils import run_bass_kernel_spmd

    nc = bacc.Bacc("TRN2", target_bir_lowering=False, num_devices=1)
    arrays = arrange(inputs)
    a = {n: nc.dram_tensor(n, v.shape, mybir.dt.from_np(v.dtype), kind="ExternalInput").ap()
         for n, v in arrays.items()}
    a["out"] = nc.dram_tensor("out", (NB, T, D), F32, kind="ExternalOutput").ap()
    decoder(nc, a)
    r = run_bass_kernel_spmd(nc, [arrays], core_ids=[0])
    return r.results[0]["out"]
```
